# Optimizing a Trainium2 kernel written in Bass

```python
import numpy as np
import jax
import jax.numpy as jnp

def _softmax(x, axis=-1):
    return jax.nn.softmax(x, axis=axis)

def _gelu(x):
    return jax.nn.gelu(x, approximate=True)

def _silu(x):
    return jax.nn.silu(x)

def _sigmoid(x):
    return jax.nn.sigmoid(x)

def _layernorm(x, axis=-1, eps=1e-05):
    m = jnp.mean(x, axis=axis, keepdims=True)
    v = jnp.var(x, axis=axis, keepdims=True)
    return (x - m) / jnp.sqrt(v + eps)

def _scatter_add(tgt, idx, src, axis=0):
    return tgt.at[idx].add(src)

def _segment_sum(src, seg, n):
    return jax.ops.segment_sum(src, seg, n)
kernel_name = 'mk_xattn_ffn_d2_seqx_r8_3f48c3'

def setup_inputs(seed: int=0):
    np.random.seed(seed)
    _w = jnp.asarray

    def _rec_inputs():
        import jax
        import jax.numpy as jnp
        _rk = jax.random.key(seed)
        x = -0.0003929 + 0.9999 * jax.random.normal(jax.random.fold_in(_rk, 1), (16, 64, 512), jnp.float32)
        _lenS = 64 - jax.random.randint(jax.random.fold_in(_rk, 7), (16,), 0, max(1, 64 // 4) + 1, jnp.int32)
        _lenS2 = 64 - jax.random.randint(jax.random.fold_in(_rk, 8), (16,), 0, max(1, 64 // 4) + 1, jnp.int32)
        _ctx_4096P = jax.random.normal(jax.random.fold_in(_rk, 11), (16, 16, 512), jnp.float32)
        _ctx_4096c = jax.random.dirichlet(jax.random.fold_in(_rk, 511), 0.3 * jnp.ones((16,), jnp.float32), (16, 64))
        _ctx_4096t = jnp.einsum('bsk,bkd->bsd', _ctx_4096c, _ctx_4096P)
        _ctx_4096t = _ctx_4096t * jax.lax.rsqrt(jnp.mean(jnp.square(_ctx_4096t)) + 1e-12) * 0.953939
        ctx_4096 = 2.81802e-05 + 1.00001 * (_ctx_4096t + 0.3 * jax.random.normal(jax.random.fold_in(_rk, 611), (16, 64, 512), jnp.float32))
        return (x, ctx_4096)
    x, ctx_4096 = _rec_inputs()

    def _L0_xattn_setup():
        import jax, jax.numpy as jnp
        import numpy as np
        EMB_DIM = 64
        HEADS = 8
        key = jax.random.key(seed)
        kq, kk, kv = jax.random.split(key, 3)
        B, C, N = (8, EMB_DIM, 512)
        q = jax.random.normal(kq, (B, C, N), dtype=jnp.float32)
        k = jax.random.normal(kk, (B, C, N), dtype=jnp.float32)
        v = jax.random.normal(kv, (B, C, N), dtype=jnp.float32)
        return {'q': q, 'k': k, 'v': v}
    _L0_xattn_all = _L0_xattn_setup()
    _L0_xattn_in = {k: v for k, v in _L0_xattn_all.items() if k in ()}
    del _L0_xattn_all

    def _L0_ffn_setup():
        import jax, jax.numpy as jnp
        import numpy as np
        HIDDEN = 512
        INTER = 1376
        RANK = 128
        B, S = (2, 256)
        key = jax.random.key(seed)
        ks = jax.random.split(key, 7)
        sc = 0.02
        return {'x': jax.random.normal(ks[0], (B, S, HIDDEN), dtype=jnp.float32), 'U1': jax.random.normal(ks[1], (HIDDEN, RANK), dtype=jnp.float32) * sc, 'V1': jax.random.normal(ks[2], (RANK, 2 * INTER), dtype=jnp.float32) * sc, 'U2': jax.random.normal(ks[3], (INTER, RANK), dtype=jnp.float32) * sc, 'V2': jax.random.normal(ks[4], (RANK, HIDDEN), dtype=jnp.float32) * sc, 'b1': jax.random.normal(ks[5], (2 * INTER,), dtype=jnp.float32) * sc, 'b2': jax.random.normal(ks[6], (HIDDEN,), dtype=jnp.float32) * sc}
    _L0_ffn_all = _L0_ffn_setup()
    _L0_ffn_in = {k: v for k, v in _L0_ffn_all.items() if k in ('U1', 'V1', 'U2', 'V2', 'b1', 'b2')}
    del _L0_ffn_all

    def _L1_xattn_setup():
        import jax, jax.numpy as jnp
        import numpy as np
        B, Q, D = (8, 64, 512)
        CTX = 512
        H, KV, HD = (16, 4, 96)
        G = H // KV
        key = jax.random.key(seed)
        ks = jax.random.split(key, 6)
        s = 0.02
        return {'latents': jax.random.normal(ks[0], (B, Q, D), jnp.float32), 'context': jax.random.normal(ks[1], (B, CTX, D), jnp.float32), 'Wq': jax.random.normal(ks[2], (H * HD, D), jnp.float32) * s, 'Wk': jax.random.normal(ks[3], (KV * HD, D), jnp.float32) * s, 'Wv': jax.random.normal(ks[4], (KV * HD, D), jnp.float32) * s, 'Wo': jax.random.normal(ks[5], (D, H * HD), jnp.float32) * s}
    _L1_xattn_all = _L1_xattn_setup()
    _L1_xattn_in = {k: v for k, v in _L1_xattn_all.items() if k in ('Wq', 'Wk', 'Wv', 'Wo')}
    del _L1_xattn_all

    def _L1_ffn_setup():
        import jax, jax.numpy as jnp
        import numpy as np
        H = 512
        I = 256
        E = 16
        TOPK = 4
        SI = 256
        key = jax.random.key(seed)
        ks = jax.random.split(key, 9)
        s = 0.02
        return {'hidden_states': jax.random.normal(ks[0], (2, 256, H), dtype=jnp.float32), 'gate_w': jax.random.normal(ks[1], (E, H), dtype=jnp.float32) * s, 'bias': jnp.zeros((E,), dtype=jnp.float32), 'Wg': jax.random.normal(ks[2], (E, I, H), dtype=jnp.float32) * s, 'Wu': jax.random.normal(ks[3], (E, I, H), dtype=jnp.float32) * s, 'Wd': jax.random.normal(ks[4], (E, H, I), dtype=jnp.float32) * s, 'Sg': jax.random.normal(ks[5], (SI, H), dtype=jnp.float32) * s, 'Su': jax.random.normal(ks[6], (SI, H), dtype=jnp.float32) * s, 'Sd': jax.random.normal(ks[7], (H, SI), dtype=jnp.float32) * s}
    _L1_ffn_all = _L1_ffn_setup()
    _L1_ffn_in = {k: v for k, v in _L1_ffn_all.items() if k in ('gate_w', 'bias', 'Wg', 'Wu', 'Wd', 'Sg', 'Su', 'Sd')}
    del _L1_ffn_all
    return {'x': x, 'ctx_4096': ctx_4096, 'L0_ffn_U1': _L0_ffn_in['U1'], 'L0_ffn_V1': _L0_ffn_in['V1'], 'L0_ffn_U2': _L0_ffn_in['U2'], 'L0_ffn_V2': _L0_ffn_in['V2'], 'L0_ffn_b1': _L0_ffn_in['b1'], 'L0_ffn_b2': _L0_ffn_in['b2'], 'L1_xattn_Wq': _L1_xattn_in['Wq'], 'L1_xattn_Wk': _L1_xattn_in['Wk'], 'L1_xattn_Wv': _L1_xattn_in['Wv'], 'L1_xattn_Wo': _L1_xattn_in['Wo'], 'L1_ffn_gate_w': _L1_ffn_in['gate_w'], 'L1_ffn_bias': _L1_ffn_in['bias'], 'L1_ffn_Wg': _L1_ffn_in['Wg'], 'L1_ffn_Wu': _L1_ffn_in['Wu'], 'L1_ffn_Wd': _L1_ffn_in['Wd'], 'L1_ffn_Sg': _L1_ffn_in['Sg'], 'L1_ffn_Su': _L1_ffn_in['Su'], 'L1_ffn_Sd': _L1_ffn_in['Sd']}

def reference(x, ctx_4096, L0_ffn_U1, L0_ffn_V1, L0_ffn_U2, L0_ffn_V2, L0_ffn_b1, L0_ffn_b2, L1_xattn_Wq, L1_xattn_Wk, L1_xattn_Wv, L1_xattn_Wo, L1_ffn_gate_w, L1_ffn_bias, L1_ffn_Wg, L1_ffn_Wu, L1_ffn_Wd, L1_ffn_Sg, L1_ffn_Su, L1_ffn_Sd):
    import jax
    import jax.numpy as jnp

    def _L0_xattn_ref(q, k, v):
        import jax, jax.numpy as jnp
        import numpy as np
        EMB_DIM = 64
        HEADS = 8
        B, C, N = q.shape
        H = HEADS
        dh = C // H
        qh = q.transpose(0, 2, 1).reshape(B, N, H, dh)
        kh = k.transpose(0, 2, 1).reshape(B, N, H, dh)
        vh = v.transpose(0, 2, 1).reshape(B, N, H, dh)
        qh = jax.nn.softmax(qh, axis=3)
        kh = jax.nn.softmax(kh, axis=1)
        kvs = jnp.einsum('bnhd,bnhe->bhde', kh, vh)
        out = jnp.einsum('bnhd,bhde->bnhe', qh, kvs)
        return out.transpose(0, 2, 3, 1).reshape(B, C, N)

    def _L0_ffn_ref(x, U1, V1, U2, V2, b1, b2):
        import jax, jax.numpy as jnp
        import numpy as np
        HIDDEN = 512
        INTER = 1376
        RANK = 128
        B, S = (2, 256)
        P = jnp.einsum('bsh,hr->bsr', x, U1)
        H = jnp.einsum('bsr,rf->bsf', P, V1) + b1
        gate, up = (H[..., :INTER], H[..., INTER:])
        act = jax.nn.silu(gate) * up
        Z = jnp.einsum('bsi,ir->bsr', act, U2)
        out = jnp.einsum('bsr,rh->bsh', Z, V2) + b2
        return out

    def _L1_xattn_ref(latents, context, Wq, Wk, Wv, Wo):
        import jax, jax.numpy as jnp
        import numpy as np
        B, Q, D = (8, 64, 512)
        CTX = 512
        H, KV, HD = (16, 4, 96)
        G = H // KV
        b, q_len, _ = latents.shape
        hidden = jnp.concatenate([context, latents], axis=1)
        s_len = hidden.shape[1]
        q = (latents @ Wq.T).reshape(b, q_len, H, HD)
        k = (hidden @ Wk.T).reshape(b, s_len, KV, HD)
        v = (hidden @ Wv.T).reshape(b, s_len, KV, HD)
        q = q.transpose(0, 2, 1, 3).reshape(b, KV, G, q_len, HD)
        k = k.transpose(0, 2, 1, 3)
        v = v.transpose(0, 2, 1, 3)
        scale = 1.0 / jnp.sqrt(jnp.asarray(HD, q.dtype))
        scores = jnp.einsum('bkgqd,bksd->bkgqs', q, k) * scale
        attn = jax.nn.softmax(scores.astype(jnp.float32), axis=-1).astype(q.dtype)
        out = jnp.einsum('bkgqs,bksd->bkgqd', attn, v)
        out = out.reshape(b, H, q_len, HD).transpose(0, 2, 1, 3).reshape(b, q_len, H * HD)
        return out @ Wo.T

    def _L1_ffn_ref(hidden_states, gate_w, bias, Wg, Wu, Wd, Sg, Su, Sd):
        import jax, jax.numpy as jnp
        import numpy as np
        H = 512
        I = 256
        E = 16
        TOPK = 4
        SI = 256
        orig_shape = hidden_states.shape
        x = hidden_states.reshape(-1, orig_shape[-1])
        scores = jax.nn.sigmoid(x @ gate_w.T) + bias
        topk_w, topk_idx = jax.lax.top_k(scores, TOPK)
        topk_w = topk_w / (jnp.sum(topk_w, axis=-1, keepdims=True) + 1e-20)
        cw = jnp.sum(jax.nn.one_hot(topk_idx, E, dtype=x.dtype) * topk_w[..., None], axis=1)
        g = jnp.einsum('th,eih->eti', x, Wg)
        u = jnp.einsum('th,eih->eti', x, Wu)
        z = jax.nn.silu(g) * u
        zw = z * cw.T[:, :, None]
        out = jnp.einsum('eti,ehi->th', zw, Wd)
        out = out + jax.nn.silu(x @ Sg.T) * (x @ Su.T) @ Sd.T
        return out.reshape(orig_shape)
    x = x + _L0_xattn_ref(_layernorm(x, axis=-1), ctx_4096, ctx_4096)
    x = x + _L0_ffn_ref(_layernorm(x, axis=-1), L0_ffn_U1, L0_ffn_V1, L0_ffn_U2, L0_ffn_V2, L0_ffn_b1, L0_ffn_b2)
    x = x + _L1_xattn_ref(_layernorm(x, axis=-1), ctx_4096, L1_xattn_Wq, L1_xattn_Wk, L1_xattn_Wv, L1_xattn_Wo)
    x = x + _L1_ffn_ref(_layernorm(x, axis=-1), L1_ffn_gate_w, L1_ffn_bias, L1_ffn_Wg, L1_ffn_Wu, L1_ffn_Wd, L1_ffn_Sg, L1_ffn_Su, L1_ffn_Sd)
    return x

_drawn_inputs = setup_inputs


def setup_inputs(seed=0):
    import zlib

    import numpy as np

    out = dict(_drawn_inputs(seed))
    spreads = {'L1_ffn_bias': (0.0, 2.0)}
    factors = {'L0_ffn_U1': 8.0,
     'L0_ffn_V1': 8.0,
     'L0_ffn_U2': 8.0,
     'L0_ffn_V2': 8.0,
     'L0_ffn_b1': 8.0,
     'L0_ffn_b2': 24.912,
     'L1_xattn_Wq': 48.888,
     'L1_xattn_Wk': 48.904,
     'L1_ffn_gate_w': 37.152,
     'L1_ffn_Wg': 29.896,
     'L1_ffn_Wu': 29.392,
     'L1_ffn_Wd': 29.304,
     'L1_xattn_Wv': 8.0,
     'L1_xattn_Wo': 8.0,
     'L1_ffn_Sg': 8.0,
     'L1_ffn_Su': 8.0,
     'L1_ffn_Sd': 8.0}
    for name, (base, spread) in spreads.items():
        noise = np.random.default_rng([zlib.crc32(name.encode()), seed]).standard_normal(out[name].shape)
        drawn = base * np.exp(spread * noise) if base else spread * noise
        out[name] = jnp.asarray(drawn.astype(out[name].dtype))
    for name, factor in factors.items():
        out[name] = (out[name] * factor).astype(out[name].dtype)
    return out
```

```python
from contextlib import ExitStack

import concourse.bass as bass
from concourse import mybir

F32 = mybir.dt.float32
I32 = mybir.dt.int32
U32 = mybir.dt.uint32
ALU = mybir.AluOpType
ACT = mybir.ActivationFunctionType
AX_X = mybir.AxisListType.X

P = 128
B, S, D = 16, 64, 512
T = B * S
J = T // P
KC = D // P
DH = 8
RANK, INTER = 128, 1376
NF = -(-INTER // P)
LASTF = INTER - (NF - 1) * P
G, HG, HD = 4, 4, 96
NQT = G * 3
E, I, TOPK = 16, 256, 4
EW = (KC + I // P) * D
TILES = T * TOPK // P + E - 1
MINTILES = T * TOPK // P + 1
RING = 4
EPS = 1e-5
SCALE = float(HD) ** -0.5


def build(nc, x_d, ctx_d, ctxT_d, cst_d, u1_d, v1_d, u2_d, v2_d, b1_d, b2_d,
          wq_d, wk_d, wv_d, wo_d, gw_d, gb_d, we_d, ws_d, out_d):
    z_d = nc.dram_tensor("z_rows", (T, D), F32, kind="Internal").ap()
    id_d = nc.dram_tensor("slot_tokens", (P, P), F32, kind="Internal").ap()
    y_d = nc.dram_tensor("expert_rows", (TILES * P, D), F32, kind="Internal").ap()

    with ExitStack() as stack:
        def sb(name, shape, dt=F32):
            return stack.enter_context(nc.sbuf_tensor(name, shape, dt))

        def sem(name):
            return stack.enter_context(nc.semaphore(name))

        xr = sb("xr", [P, J, D])
        cst = sb("cst", [P, 4 * P + 176])
        zT = sb("zT", [P, KC, T])
        r1 = sb("r1", [P, 8192])
        r3 = sb("r3", [P, 6144])
        r4 = sb("r4", [P, 3072])
        rq = sb("rq", [P, 8192])
        kv = sb("kv", [P, 14336])
        zrow = sb("zrow", [P, 2, D])

        ident, blk8, tri, ones = (cst[:, i * P:(i + 1) * P] for i in range(4))
        c0 = 4 * P
        iota16 = cst[:, c0:c0 + 16]
        iota16x8 = cst[:, c0 + 16:c0 + 32]
        iota16c = cst[:, c0 + 32:c0 + 48]
        m128 = cst[:, c0 + 48:c0 + 56]
        ringo = cst[:, c0 + 56:c0 + 72]
        iota48 = cst[:, c0 + 72:c0 + 120]
        even24 = cst[:, c0 + 120:c0 + 144]
        tokid = cst[:, c0 + 144:c0 + 152]
        ctxT = r1[:, 0:4096].rearrange("p (k t) -> p k t", k=KC)
        crow = r1[:, 4096:8192].rearrange("p (j d) -> p j d", j=J)
        wq = r1[:, 0:6144].rearrange("p (k m) -> p k m", k=KC)
        prob = r1[:, 6144:7168].rearrange("p (n u s) -> p n u s", n=2, u=4)
        probT = r1[:, 7168:8192].rearrange("p (n c) -> p n c", n=2)
        u1 = r3[:, 0:512].rearrange("p (k r) -> p k r", k=KC)
        v1 = r3[:, 512:512 + 2 * INTER]
        u2 = r3[:, 3264:3264 + NF * RANK].rearrange("p (c r) -> p c r", c=NF)
        v2 = r3[:, 4672:5184]
        b2 = r3[:, 5184:5696]
        b1 = r3[:, 5696:5696 + 2 * NF]
        wo = r3[:, 0:6144].rearrange("p (m d) -> p m d", m=NQT)
        ek = r4[:, 0:1024].rearrange("p (n d) -> p n d", n=2)
        eq = r4[:, 1024:2048].rearrange("p (n d) -> p n d", n=2)
        ekT = r4[:, 2048:3072].rearrange("p (n c) -> p n c", n=2)
        oT = r4[:, 0:3072].rearrange("p (n m t) -> p n m t", n=2, m=NQT)
        qT = rq[:, :].rearrange("p (n b h s) -> p n b h s", n=2, b=4, h=G * HG)
        hs = rq[:, 0:1024].rearrange("p (n t) -> p n t", n=2)
        ha = rq[:, 1024:2048].rearrange("p (n t) -> p n t", n=2)
        pT = rq[:, 2048:2560]
        oz = rq[:, 2560:3072]
        srec = rq[:, 3072:3584]
        sout = rq[:, 3584:4096]
        wk = rq[:, 4096:4096 + KC * G * HD].rearrange("p (k m) -> p k m", k=KC)
        wv = rq[:, 5632:5632 + KC * G * HD].rearrange("p (k m) -> p k m", k=KC)
        kT = kv[:, 0:8192].rearrange("p (g b s) -> p g b s", g=G, b=B)
        v = kv[:, 8192:14336].rearrange("p (b c) -> p b c", b=B)
        ering = kv[:, 0:RING * EW]
        wsh = r1[:, 0:EW]
        xrow = rq[:, 0:1024].rearrange("p (n d) -> p n d", n=2)
        xT = rq[:, 1024:2048].rearrange("p (n c) -> p n c", n=2)
        sg = rq[:, 2048:2560].rearrange("p (n i) -> p n i", n=2)
        zg = rq[:, 2560:3072].rearrange("p (n i) -> p n i", n=2)
        zgT = rq[:, 3072:3584].rearrange("p (n i) -> p n i", n=2)
        yrow = rq[:, 3584:4608].rearrange("p (n d) -> p n d", n=2)
        NY = 6
        ygot = r3[:, 0:NY * D].rearrange("p (n d) -> p n d", n=NY)

        kvm = sb("kvm", [P, 2, P])
        gw = sb("gw", [P, KC, E])
        gb = sb("gb", [P, E])
        zero = sb("zero", [P, P])
        half = sb("half", [P, 1])
        st = sb("st", [P, 2, 6])
        mv = sb("mv", [P, 4 * J, 2])
        ve = sb("ve", [P, 4 * J])
        rstd = sb("rstd", [P, 4 * J])
        nmr = sb("nmr", [P, J])
        cmx = sb("cmx", [P, J])
        ncm = sb("ncm", [P, J])
        ksum = sb("ksum", [P, J])
        krec = sb("krec", [P, J])
        smx = sb("smx", [P, 4, 4])
        snm = sb("snm", [P, 4, 4])
        ssum = sb("ssum", [P, 4, 4])
        srs = sb("srs", [P, 4, 4])
        gsc = sb("gsc", [P, 4, E])
        top8 = sb("top8", [P, 8])
        idx8 = sb("idx8", [P, 8], U32)
        idxf = sb("idxf", [P, 8])
        onehot = sb("onehot", [P, J, TOPK, E])
        mask = sb("mask", [P, J, E])
        mcum = sb("mcum", [P, J + 1, E])
        pos = sb("pos", [P, J, E])
        slot = sb("slot", [P, E])
        ohs = sb("ohs", [P, TOPK, E])
        slotf = sb("slotf", [P, TOPK])
        sloti = sb("sloti", [P, J, TOPK], I32)
        wsum = sb("wsum", [P, 1])
        wtop = sb("wtop", [P, J, TOPK])
        yif = sb("yif", [P, J, TOPK])
        yidx = sb("yidx", [P, J, TOPK], I32)
        tb = sb("tb", [P, 12, E])
        tt = r4[:, 0:3 * 48 * E].rearrange("p (n c) -> p n c", n=3)
        tf = sb("tf", [P, 3 * 48 + 3 * E + 2])
        tab = sb("tab", [P, 3 * 48 + 3 * E + 2], I32)
        idrow = sb("idrow", [P, P])
        ids = sb("ids", [P, P], I32)
        gidx = sb("gidx", [P, 2], I32)

        ps = stack.enter_context(nc.psum_tensor("ps", [P, 8, 512], F32))

        s_cst = sem("identity_and_blocks_loaded")
        s_tables = sem("count_constants_loaded")
        s_c = [sem(f"context_rows_loaded{j}") for j in range(J)]
        s_x = [sem(f"x_rows_loaded{j}") for j in range(J)]
        s_wk = sem("wk_loaded")
        s_wv = sem("wv_loaded")
        s_ct = [sem(f"ctxT_loaded{h}") for h in range(J // 2)]
        s_ffw = sem("ffn_weights_loaded")
        s_small = sem("gate_weights_loaded")
        s_wq = sem("wq_loaded")
        s_wo = sem("wo_loaded")
        s_ws = sem("shared_weights_loaded")
        s_ms = sem("memsets_done")
        s_idz = sem("slot_table_zeroed")
        s_yz = sem("result_rows_zeroed")
        chain_v = sem("vector_chain")
        chain_p = sem("pool_chain")
        s_stat = sem("stats_done")
        s_rstd = sem("rstd_done")
        s_ncm = sem("ctx_negmax_done")
        s_nmr = sem("x_shift_done")
        s_ek = sem("exp_k_done")
        s_eq = sem("exp_q_done")
        s_tr = sem("transposes_done")
        s_trc = sem("transposes_copied")
        s_kvs = sem("kvs_done")
        s_kvm = sem("kvs_masked")
        s_a = sem("first_attention_done")
        s_ac = sem("first_attention_scaled")
        s_x1 = sem("x1_done")
        s_z = sem("z_done")
        s_xb = sem("x1_plus_b2_done")
        s_pr = sem("kv_projection_done")
        s_prc = sem("kv_projection_copied")
        s_pt = sem("rank_in_done")
        s_ptc = sem("rank_in_copied")
        s_gu = sem("ffn_gate_up_done")
        s_sil = sem("ffn_silu_done")
        s_act = sem("ffn_act_done")
        s_oz = sem("rank_out_done")
        s_ozc = sem("rank_out_copied")
        s_fo = sem("ffn_rows_done")
        s_x2 = sem("x2_done")
        s_q = sem("q_done")
        s_qca = sem("q_copied_act")
        s_qcv = sem("q_copied_dve")
        s_s = sem("scores_done")
        s_snm = sem("score_negmax_done")
        s_p = sem("exp_done")
        s_pn = sem("probs_done")
        s_o = sem("pv_done")
        s_oc = sem("pv_copied")
        s_op = sem("o_projection_done")
        s_x3 = sem("x3_done")
        s_zd = sem("z_rows_stored")
        s_g = sem("gate_logits_done")
        s_ge = sem("gate_exp_done")
        s_mk = sem("expert_mask_done")
        s_ps = sem("positions_done")
        s_tot = sem("expert_counts_done")
        s_yi = sem("result_rows_known")
        s_sl = sem("slots_done")
        s_sc = [sem(f"ids_scattered{k}") for k in range(TOPK)]
        s_tabl = sem("load_table_done")
        s_tabc = sem("tile_columns_done")
        s_tab = sem("tile_weights_done")
        s_idl = sem("slot_tokens_loaded")
        s_idt = sem("slot_tokens_transposed")
        s_ids = sem("slot_tokens_ready")
        s_hg = sem("shared_gate_up_done")
        s_hsil = sem("shared_silu_done")
        s_hz = sem("shared_act_done")
        s_ht = sem("shared_act_transposed")
        s_htc = sem("shared_act_copied")
        s_hd = sem("shared_down_done")
        s_x4 = sem("x4_done")
        s_wdma = [sem(f"expert_weights_dma{i}") for i in range(2)]
        s_w = sem("expert_weights_ready")
        s_gi = sem("gather_index_ready")
        s_giw = sem("pool_waits_passed")
        s_gx = [sem(f"rows_gathered{i}") for i in range(2)]
        s_tx = sem("rows_transposed")
        s_txc = sem("rows_copied")
        s_eg = sem("expert_gate_up_done")
        s_esil = sem("expert_silu_done")
        s_ez = sem("expert_act_done")
        s_tz = sem("act_transposed")
        s_tzc = sem("act_copied")
        s_ed = sem("expert_down_done")
        s_yc = sem("expert_rows_copied")
        s_ys = [sem(f"expert_rows_stored{i}") for i in range(2)]
        s_yg = [sem(f"expert_rows_gathered{i}") for i in range(NY)]
        s_cmb = sem("combine_steps_done")
        s_out = sem("output_stored")

        ctx_units = []
        for h in range(2):
            ctx_units += [("v", j, 0) for j in range(4 * h, 4 * h + 4)]
            ctx_units += [("k", t, h, 0) for t in range(3)]
        lat_units = []
        for h in range(2):
            lat_units.append([("k", t, h, 1) for t in range(3)] + [("v", j, 1) for j in range(4 * h, 4 * h + 4)])

        prog = []
        fill = list(ctx_units)
        prog += [("a_stat", 0), ("a_stat", 1)]
        per_step = (1, 2, 1, 2, 2, 2, 1, 2, 1, 0)
        prog.append(("a_prep", 0))
        for s in range(J + 2):
            if s < J:
                prog.append(("a_t", s))
            if 2 <= s:
                prog.append(("a_out", s - 2))
                prog.append(("x1", s - 2))
            if s + 1 < J:
                prog.append(("a_prep", s + 1))
            if 1 <= s <= J:
                prog.append(("a_q", s - 1))
            if s + 2 < J:
                prog.append(("a_stat", s + 2))
            if 4 <= s:
                prog.append(("ln_z", 1, s - 4))
            if per_step[s]:
                prog.append(("kv", fill.pop(0)))
            if 1 <= s <= J:
                prog.append(("a_kvs", s - 1))
            if 3 <= s:
                prog.append(("ln_stat", 1, s - 3))
            if per_step[s] > 1:
                prog.append(("kv", fill.pop(0)))
            if 4 <= s:
                prog.append(("ln_t", 1, s - 4))
        for h in range(2):
            prog.append(("f_in", h))
            beside = {0: [(1, 6), (1, 7)], 1: [(2, j) for j in range(4)]}[h]
            for c in range(NF):
                prog.append(("f_gu", h, c))
                if c:
                    prog.append(("f_z", h, c - 1))
                i = c // 2
                if c % 2 == 0 and i < len(beside):
                    if beside[i] != (1, 6):
                        prog.append(("ln_stat", *beside[i]))
                if c % 2 == 1 and i < len(beside):
                    prog.append(("ln_z", *beside[i]))
                if c % 2 == 0 and 1 <= i <= len(beside):
                    prog.append(("ln_t", *beside[i - 1]))
            prog.append(("f_z", h, NF - 1))
            for j in range(4 * h, 4 * h + 4):
                prog.append(("f_out", j))
        for i, u in enumerate(lat_units[0]):
            if i < 4:
                prog.append(("ln_stat", 2, 4 + i))
            prog.append(("kv", u))
            if i < 4:
                prog.append(("ln_z", 2, 4 + i))
            if 1 <= i < 5:
                prog.append(("ln_t", 2, 3 + i))
        for u in lat_units[1]:
            prog.append(("kv", u))
        for g in range(G):
            prog.append(("q", 0, g))
        NU = 2 * B
        for n in range(NU + 1):
            if n < NU:
                prog.append(("s", n))
            q, r = n // 8, n % 8
            if q < 3 and r % 2 == 0:
                prog.append(("q", q + 1, r // 2))
            for off, what in ((6, ("op0",)), (7, ("op1",)), (9, ("ln_stat", 3)), (10, ("ln_z", 3)),
                              (11, ("ln_t", 3)), (12, ("gate",)), (13, ("place",))):
                j, m = divmod(n - off, 4)
                if m == 0 and 0 <= j < J:
                    prog.append((*what, j))
            if 1 <= n <= NU:
                prog.append(("t", n - 1))
            if 2 <= n <= NU + 1:
                prog.append(("pv", n - 2))
            if n < NU:
                prog.append(("pn", n))
        prog += [("ln_stat", 3, J - 2), ("place", J - 3), ("sh_gu", 0), ("pv", NU - 1), ("ln_z", 3, J - 2), ("sh_t", 0),
                 ("op0", J - 1), ("op1", J - 1), ("ln_t", 3, J - 2), ("ln_stat", 3, J - 1), ("ln_z", 3, J - 1),
                 ("sh_gu", 1), ("gate", J - 2), ("ln_t", 3, J - 1), ("sh_d", 0), ("sh_t", 1), ("place", J - 2),
                 ("sh_gu", 2), ("gate", J - 1), ("sh_d", 1), ("sh_t", 2), ("sh_gu", 3), ("place", J - 1),
                 ("sh_d", 2), ("sh_t", 3), ("route", 0), ("sh_gu", 4), ("sh_d", 3), ("route", 1), ("sh_t", 4),
                 ("sh_gu", 5), ("sh_d", 4), ("route", 2), ("sh_t", 5), ("ids",), ("sh_gu", 6), ("sh_d", 5),
                 ("sh_t", 6), ("sh_gu", 7), ("sh_d", 6), ("sh_t", 7), ("sh_d", 7), ("route", 3)]

        def order(kinds):
            return {step: i for i, step in enumerate(p for p in prog if p[0] in kinds)}

        TRN = order(("a_t", "ln_t", "t"))
        KVN = order(("kv",))
        LNN = order(("ln_z",))
        STN = order(("a_stat", "ln_stat"))
        block = stack.enter_context(nc.Block())

        def halves(unit):
            return slice(S * unit[-1], S * unit[-1] + S)

        @block.sync
        def _(sp):
            sp.dma_start(crow[:, 0, :], ctx_d[0:P, :]).then_inc(s_c[0], 16)
            sp.dma_start(cst[:, 0:2 * P], cst_d[:, 0:2 * P]).then_inc(s_cst, 16)
            for j in range(J):
                if j:
                    sp.dma_start(crow[:, j, :], ctx_d[j * P:(j + 1) * P, :]).then_inc(s_c[j], 16)
                sp.dma_start(xr[:, j, :], x_d[j * P:(j + 1) * P, :]).then_inc(s_x[j], 16)
                if j in (2, 4):
                    h = j // 2 + 1
                    sp.dma_start(ctxT[:, :, h * 256:(h + 1) * 256], ctxT_d[:, :, h * 256:(h + 1) * 256]).then_inc(s_ct[h], 16)
            sp.dma_start(u1, u1_d.rearrange("p (k r) -> p k r", k=KC)).then_inc(s_ffw, 16)
            sp.dma_start(v1, v1_d).then_inc(s_ffw, 16)
            sp.dma_start(u2, u2_d.rearrange("p (c r) -> p c r", c=NF)).then_inc(s_ffw, 16)
            sp.dma_start(v2, v2_d).then_inc(s_ffw, 16)
            sp.dma_start(b1, b1_d).then_inc(s_ffw, 16)
            sp.dma_start(b2, b2_d.to_broadcast((P, D))).then_inc(s_ffw, 16)
            sp.dma_start(gw[:, :, :], gw_d.rearrange("p (k e) -> p k e", k=KC)).then_inc(s_small, 16)
            sp.dma_start(gb[:, :], gb_d.to_broadcast((P, E))).then_inc(s_small, 16)
            sp.dma_start(cst[:, 2 * P:], cst_d[:, 2 * P:]).then_inc(s_tables, 16)
            sp.wait_ge(s_ms, 2)
            sp.dma_start(id_d, zero[:, :]).then_inc(s_idz, 16)
            for i in range(MINTILES, TILES):
                sp.dma_start(y_d[i * P:(i + 1) * P, :].rearrange("p (a c) -> p a c", c=P),
                             zero[:, :].rearrange("p (a c) -> p a c", a=1).to_broadcast((P, D // P, P)))\
                    .then_inc(s_yz, 16)
            sp.wait_ge(s_a, J)
            sp.wait_ge(s_ek, J)
            sp.wait_ge(s_ncm, J)
            sp.wait_ge(s_pr, len(ctx_units))
            sp.dma_start(wq, wq_d.rearrange("p (k m) -> p k m", k=KC)).then_inc(s_wq, 16)
            sp.wait_ge(s_fo, J)
            sp.wait_ge(s_xb, J)
            sp.wait_ge(s_act, 2 * NF)
            sp.dma_start(wo, wo_d.rearrange("p (m d) -> p m d", m=NQT)).then_inc(s_wo, 16)
            for j in range(J):
                if j == 3:
                    sp.wait_ge(s_q, 4 * G)
                    sp.dma_start(wsh, ws_d).then_inc(s_ws, 16)
                sp.wait_ge(s_z, LNN[("ln_z", 3, j)] + 1)
                sp.dma_start(z_d[j * P:(j + 1) * P, :], zrow[:, LNN[("ln_z", 3, j)] % 2, :]).then_inc(s_zd, 16)
                sp.wait_ge(s_zd, 16 * (j + 1))
            sp.wait_ge(s_tabl, 1)
            sp.wait_ge(s_o, NU)
            loads = sp.value_load(tab[0:1, 192:193], min_val=1, max_val=E)
            first = sp.value_load(tab[0:1, 144:145], min_val=0, max_val=E - 1)
            sp.dma_start(ering[:, 0:EW], we_d[bass.ds(first, 1), :, :].rearrange("a p n -> (a p) n")).then_inc(s_wdma[0], 16)
            sp.wait_ge(s_wdma[0], 16)
            sp.sem_inc(s_w, 1)
            with sp.Fori(1, loads) as o:
                expert = sp.value_load(tab[0:1, bass.ds(o + 144, 1)], min_val=0, max_val=E - 1)
                free = sp.value_load(tab[0:1, bass.ds(o + 160, 1)], min_val=0, max_val=TILES)
                at = sp.value_load(tab[0:1, bass.ds(o + 176, 1)], min_val=0, max_val=(RING - 1) * EW)
                sp.wait_ge(s_ed, free + 1)
                sp.dma_start(ering[:, bass.ds(at, EW)],
                             we_d[bass.ds(expert, 1), :, :].rearrange("a p n -> (a p) n")).then_inc(s_wdma[1], 16)
                sp.wait_ge(s_wdma[1], 16 * o)
                sp.sem_inc(s_w, 1)
            for j in range(J):
                sp.wait_ge(s_cmb, TOPK * (j + 1))
                sp.dma_start(out_d[j * P:(j + 1) * P, :], xr[:, j, :]).then_inc(s_out, 16)
            sp.wait_ge(s_out, 16 * J)

        @block.gpsimd
        def _(pool):
            def link(ins, n=[0]):
                n[0] += 1
                ins.then_inc(chain_p, 1)
                pool.wait_ge(chain_p, n[0])

            pool.memset(half[:, :], -0.5).then_inc(s_ms, 1)
            pool.memset(zero[:, :], 0.0).then_inc(s_ms, 1)
            pool.memset(mcum[:, 0, :], 0.0).then_inc(s_ms, 1)
            pool.wait_ge(s_ms, 1)
            stats = [0]

            def root(col):
                stats[0] += 1
                pool.wait_ge(s_stat, stats[0])
                link(pool.tensor_scalar(ve[:, col:col + 1], mv[:, col, 1:2], EPS, None, ALU.add))
                pool.tensor_tensor(rstd[:, col:col + 1], ve[:, col:col + 1], half[:, :], ALU.pow).then_inc(s_rstd, 1)

            for step in prog:
                if step[0] == "a_stat":
                    root(step[1])
                elif step[0] == "x1":
                    j = step[1]
                    pool.wait_ge(s_ac, j + 1)
                    pool.tensor_tensor(xr[:, j, :], xr[:, j, :], sout, ALU.add).then_inc(s_x1, 1)
                elif step[0] == "ln_stat":
                    root(J * step[1] + step[2])
                elif step[0] == "ln_z" and step[1] == 1:
                    j = step[2]
                    if j == 0:
                        pool.wait_ge(s_ffw, 6 * 16)
                    pool.wait_ge(s_z, LNN[step] + 1)
                    pool.tensor_tensor(xr[:, j, :], xr[:, j, :], b2, ALU.add).then_inc(s_xb, 1)
                elif step[0] == "place":
                    j = step[1]
                    pool.wait_ge(s_sl, j + 1)
                    pool.wait_ge(s_idz, 16)
                    pool.wait_ge(s_tables, 16)
                    for k in range(TOPK):
                        if j:
                            pool.wait_ge(s_sc[k], 16 * j)
                        pool.indirect_dma_start(
                            out=id_d.rearrange("a (b c) -> (a b) c", c=1),
                            out_offset=bass.IndirectOffsetOnAxis(ap=sloti[:, j, k:k + 1], axis=0),
                            in_=tokid[:, j:j + 1], in_offset=None).then_inc(s_sc[k], 16)
            for k in range(TOPK):
                pool.wait_ge(s_sc[k], 16 * J)
            pool.dma_start(idrow[:, :], id_d).then_inc(s_idl, 16)
            pool.wait_ge(s_tabl, 1)
            pool.wait_ge(s_tabc, 1)
            pool.wait_ge(s_ids, 1)
            pool.wait_ge(s_zd, 16 * J)

            def gather(i, par, wait_rows, n):
                col = pool.value_load(tab[0:1, bass.ds(i, 1)], min_val=0, max_val=P - 1)
                if wait_rows is not None:
                    pool.wait_ge(s_tx, wait_rows)
                    pool.wait_ge(s_gx[par], n * 16)
                pool.tensor_copy(gidx[:, par:par + 1], ids[:, bass.ds(col, 1)]).then_inc(s_gi, 1)
                pool.wait_ge(s_gi, i + 1)
                pool.sem_inc(s_giw, 1)
                pool.indirect_dma_start(out=xrow[:, par, :], out_offset=None, in_=z_d,
                                        in_offset=bass.IndirectOffsetOnAxis(ap=gidx[:, par:par + 1], axis=0),
                                        ).then_inc(s_gx[par], 16)

            gather(0, 0, None, 0)
            gather(1, 1, None, 0)
            pairs = pool.value_load(tab[0:1, 193:194], min_val=1, max_val=TILES // 2)
            with pool.Fori(0, pairs) as n:
                gather(2 * n + 2, 0, 2 * n + 1, n + 1)
                gather(2 * n + 3, 1, 2 * n + 2, n + 1)
            pool.wait_ge(s_ys[0], pairs * 16 + 16)
            pool.wait_ge(s_ys[1], pairs * 16)
            pool.sem_inc(s_giw, 1)
            pool.wait_ge(s_yi, 1)
            for m in range(J * TOPK):
                j, k = divmod(m, TOPK)
                if m >= NY:
                    pool.wait_ge(s_cmb, m - NY + 1)
                pool.indirect_dma_start(out=ygot[:, m % NY, :], out_offset=None, in_=y_d,
                                        in_offset=bass.IndirectOffsetOnAxis(ap=yidx[:, j, k:k + 1], axis=0),
                                        ).then_inc(s_yg[m % NY], 16)

        @block.scalar
        def _(act):
            act.dma_start(wv, wv_d.rearrange("p (k m) -> p k m", k=KC)).then_inc(s_wv, 16)
            for h in range(2):
                act.dma_start(ctxT[:, :, h * 256:(h + 1) * 256], ctxT_d[:, :, h * 256:(h + 1) * 256]).then_inc(s_ct[h], 16)
                if h == 0:
                    act.dma_start(wk, wk_d.rearrange("p (k m) -> p k m", k=KC)).then_inc(s_wk, 16)
            def copied(step, dst):
                n = TRN[step]
                act.wait_ge(s_tr, n + 1)
                act.copy(dst, ps[:, n % 2, :] if len(dst.shape) == 2 else
                         ps[:, n % 2, :].rearrange("p (k t) -> p k t", k=KC)).then_inc(s_trc, 1)

            ez = [0]
            for step in prog:
                kind = step[0]
                if kind == "a_prep":
                    j = step[1]
                    act.wait_ge(s_c[j], 16)
                    act.wait_ge(s_ncm, j + 1)
                    if j >= 2:
                        act.wait_ge(s_tr, TRN[("a_t", j - 2)] + 1)
                    act.activation(ek[:, j % 2, :], crow[:, j, :], ACT.Exp, bias=ncm[:, j:j + 1],
                                   accum_out=ksum[:, j:j + 1]).then_inc(s_ek, 1)
                elif kind == "a_q":
                    j = step[1]
                    act.wait_ge(s_x[j], 16)
                    act.wait_ge(s_nmr, j + 1)
                    if j >= 2:
                        act.wait_ge(s_a, j - 1)
                    act.activation(eq[:, j % 2, :], xr[:, j, :], ACT.Exp, bias=nmr[:, j:j + 1],
                                   scale=rstd[:, j:j + 1]).then_inc(s_eq, 1)
                elif kind == "a_t":
                    j = step[1]
                    if j >= 2:
                        act.wait_ge(s_kvs, j - 1)
                    copied(step, ekT[:, j % 2, :])
                elif kind == "ln_t":
                    copied(step, zT[:, :, step[2] * P:(step[2] + 1) * P])
                elif kind == "kv":
                    unit = step[1]
                    n = KVN[step]
                    bank = ps[:, 6 + n % 2, :]
                    act.wait_ge(s_pr, n + 1)
                    if unit[0] == "k":
                        _, t, h, _ = unit
                        bs = slice(8 * h, 8 * h + 8)
                        act.copy(kT[0:HD, t, bs, halves(unit)],
                                 bank[0:HD, :].rearrange("p (b s) -> p b s", b=8))
                        act.copy(kT[32 * t:32 * t + 32, 3, bs, halves(unit)],
                                 bank[HD:P, :].rearrange("p (b s) -> p b s", b=8)).then_inc(s_prc, 1)
                    else:
                        j = unit[1]
                        act.copy(v[halves(unit), 2 * j, :], bank[0:S, 0:G * HD])
                        act.copy(v[halves(unit), 2 * j + 1, :], bank[S:P, 0:G * HD]).then_inc(s_prc, 1)
                elif kind == "f_in":
                    h = step[1]
                    act.wait_ge(s_pt, h + 1)
                    act.copy(pT, ps[:, 7, :]).then_inc(s_ptc, 1)
                elif kind == "f_gu":
                    _, h, c = step
                    n = h * NF + c
                    m = P if c < NF - 1 else LASTF
                    if n == 0:
                        act.wait_ge(s_ffw, 6 * 16)
                    if n >= 2:
                        act.wait_ge(s_act, n - 1)
                    act.wait_ge(s_gu, n + 1)
                    act.activation(hs[0:m, n % 2, :], ps[0:m, 2 + n % 2, :], ACT.Silu,
                                   bias=b1[0:m, c:c + 1]).then_inc(s_sil, 1)
                elif kind == "f_out" and step[1] % 4 == 0:
                    act.wait_ge(s_oz, step[1] // 4 + 1)
                    act.copy(oz, ps[:, 6, :]).then_inc(s_ozc, 1)
                elif kind == "q":
                    _, q, g = step
                    act.wait_ge(s_q, 4 * q + g + 1)
                    act.copy(qT[0:HD, q % 2, :, 4 * g:4 * g + 3, :].rearrange("p b h s -> p h b s"),
                             ps[0:HD, 4:6, :].rearrange("p a b -> p (a b)")[:, 0:768]
                             .rearrange("p (h b s) -> p h b s", h=3, b=4)).then_inc(s_qca, 1)
                elif kind == "s":
                    n = step[1]
                    act.wait_ge(s_snm, n + 1)
                    if n >= 2:
                        act.wait_ge(s_tr, TRN[("t", n - 2)] + 1)
                    for u in range(4):
                        e = act.activation(prob[:, n % 2, u, :], ps[:, 2 + n % 2, u * P:(u + 1) * P], ACT.Exp,
                                           bias=snm[:, n % 4, u:u + 1], scale=SCALE,
                                           accum_out=ssum[:, n % 4, u:u + 1])
                    e.then_inc(s_p, 1)
                elif kind == "t":
                    n = step[1]
                    if n >= 2:
                        act.wait_ge(s_o, n - 1)
                    copied(step, probT[:, n % 2, :])
                elif kind == "gate":
                    j = step[1]
                    act.wait_ge(s_g, j + 1)
                    act.activation(gsc[:, 0, :], ps[:, 7, 0:E], ACT.Exp, scale=-1.0).then_inc(s_ge, 1)
                elif kind == "sh_gu":
                    j = step[1]
                    act.wait_ge(s_hg, j + 1)
                    act.activation(sg[:, j % 2, :], ps[:, 4 - 2 * (j % 2), 0:I], ACT.Silu).then_inc(s_hsil, 1)
                elif kind == "sh_t":
                    j = step[1]
                    act.wait_ge(s_ht, j + 1)
                    act.copy(zgT[:, j % 2, :], ps[:, 3, 0:I]).then_inc(s_htc, 1)
                elif kind == "ids":
                    act.wait_ge(s_idt, 1)
                    act.copy(ids[:, :], ps[:, 0, 0:P]).then_inc(s_ids, 1)

            def x_copy(i, par):
                act.wait_ge(s_tx, i + 1)
                act.copy(xT[:, par, :], ps[:, par, :]).then_inc(s_txc, 1)

            def z_copy(i, par):
                act.wait_ge(s_tz, i + 1)
                act.copy(zgT[:, par, :], ps[:, 2 + par, 0:I]).then_inc(s_tzc, 1)

            def silu(i, par):
                act.wait_ge(s_eg, i + 1)
                act.activation(sg[:, par, :], ps[:, 4 + par, 0:I], ACT.Silu).then_inc(s_esil, 1)

            def store(i, par):
                act.wait_ge(s_yc, i + 1)
                act.dma_start(y_d[bass.ds(i * P, P), :], yrow[:, par, :]).then_inc(s_ys[par], 16)

            act.wait_ge(s_tabl, 1)
            act.wait_ge(s_yz, 16 * (TILES - MINTILES))
            pairs = act.value_load(tab[0:1, 193:194], min_val=16, max_val=TILES // 2)

            def act_step(i, par):
                x_copy(i + 1, 1 - par)
                if not isinstance(i, int) or i:
                    z_copy(i - 1, 1 - par)
                silu(i, par)
                if not isinstance(i, int) or i:
                    store(i - 1, 1 - par)

            x_copy(0, 0)
            for i in range(3):
                act_step(i, i % 2)
            with act.Fori(1, 2 * pairs - 2, 2) as n:
                act_step(n + 2, 1)
                act_step(n + 3, 0)
            z_copy(2 * pairs, 0)
            store(2 * pairs, 0)

        @block.vector
        def _(dve):
            count = [0]

            def link(ins):
                count[0] += 1
                ins.then_inc(chain_v, 1)
                dve.wait_ge(chain_v, count[0])

            def probs(n):
                dve.wait_ge(s_p, n + 1)
                link(dve.reciprocal(srs[:, n % 4, :], ssum[:, n % 4, :]))
                dve.tensor_tensor(prob[:, n % 2, :, :], prob[:, n % 2, :, :],
                                  srs[:, n % 4, :].rearrange("p (u a) -> p u a", a=1).to_broadcast((P, 4, P)),
                                  ALU.mult).then_inc(s_pn, 1)

            def pick(row, j, to):
                link(dve.tensor_tensor(ohs[:, :, :], onehot[:, j, :, :],
                                       row.rearrange("p (a e) -> p a e", a=1).to_broadcast((P, TOPK, E)), ALU.mult))
                link(dve.tensor_reduce(to, ohs[:, :, :], AX_X, ALU.add))

            nE, nt, used, endT, startT, ordi, ordx, aff, one, tmp = (tb[:, i, :] for i in range(10))

            def rows(a, n):
                return a.rearrange("p (a e) -> p a e", a=1).to_broadcast((P, n, E))

            def cols(a, n):
                return a.rearrange("p (n a) -> p n a", a=1).to_broadcast((P, n, E))

            def grid(i, n):
                return tt[:, i, 0:n * E].rearrange("p (n e) -> p n e", e=E)

            def route(part):
                if part == 0:
                    route_loads()
                elif part == 1:
                    route_tiles()
                elif part == 2:
                    route_weights()
                else:
                    route_results()

            def route_loads():
                dve.wait_ge(s_tot, 1)
                link(dve.tensor_copy(nE, ps[:, 7, 0:E]))
                link(dve.memset(one, 1.0))
                g8 = tt[:, 0, 0:E * 8].rearrange("p (e m) -> p e m", m=8)
                link(dve.tensor_tensor(g8, nE.rearrange("p (e a) -> p e a", a=1).to_broadcast((P, E, 8)),
                                       m128.rearrange("p (a m) -> p a m", a=1).to_broadcast((P, E, 8)), ALU.is_gt))
                link(dve.tensor_reduce(nt, g8, AX_X, ALU.add))
                link(dve.tensor_scalar(used, nt, 0.0, None, ALU.is_gt))
                link(dve.tensor_tensor_scan(endT, one, nt, 0.0, ALU.mult, ALU.add))
                link(dve.tensor_tensor_scan(ordi, one, used, 0.0, ALU.mult, ALU.add))
                link(dve.tensor_tensor(startT, endT, nt, ALU.subtract))
                link(dve.tensor_tensor(ordx, ordi, used, ALU.subtract))
                link(dve.tensor_tensor(aff, iota16x8, startT, ALU.subtract))
                link(dve.tensor_tensor(grid(0, E), rows(ordx, E), cols(iota16, E), ALU.is_equal))
                link(dve.tensor_tensor(grid(0, E), grid(0, E), rows(used, E), ALU.mult))
                link(dve.tensor_tensor(grid(0, E), grid(0, E), rows(iota16, E), ALU.mult))
                link(dve.tensor_reduce(tf[:, 144:160], grid(0, E), AX_X, ALU.add))
                link(dve.tensor_scalar(tmp, ordx, float(RING), None, ALU.add))
                link(dve.tensor_tensor(grid(1, E), rows(tmp, E), cols(iota16, E), ALU.is_equal))
                link(dve.tensor_tensor(tmp, endT, used, ALU.mult))
                link(dve.tensor_tensor(grid(1, E), grid(1, E), rows(tmp, E), ALU.mult))
                link(dve.tensor_reduce(tf[:, 160:176], grid(1, E), AX_X, ALU.add))
                link(dve.tensor_copy(tf[:, 176:192], ringo))
                link(dve.tensor_copy(tf[:, 192:193], ordi[:, E - 1:E]))
                link(dve.tensor_scalar(tt[:, 2, 0:24], even24, endT[:, E - 1:E], None, ALU.is_le))
                link(dve.tensor_reduce(tf[:, 193:194], tt[:, 2, 0:24], AX_X, ALU.add))
                dve.tensor_copy(tab[:, 144:194], tf[:, 144:194]).then_inc(s_tabl, 1)

            def route_tiles():
                link(dve.tensor_tensor(grid(0, 48), rows(startT, 48), cols(iota48, 48), ALU.is_le))
                link(dve.tensor_tensor(grid(1, 48), rows(endT, 48), cols(iota48, 48), ALU.is_gt))
                link(dve.tensor_tensor(grid(1, 48), grid(0, 48), grid(1, 48), ALU.mult))
                link(dve.tensor_tensor(grid(2, 48), rows(aff, 48), cols(iota48, 48), ALU.add))
                link(dve.tensor_tensor(grid(2, 48), grid(2, 48), grid(1, 48), ALU.mult))
                link(dve.tensor_reduce(tf[:, 0:48], grid(2, 48), AX_X, ALU.add))
                dve.tensor_copy(tab[:, 0:48], tf[:, 0:48]).then_inc(s_tabc, 1)

            def route_weights():
                link(dve.tensor_tensor(grid(0, 48), grid(0, 48), rows(used, 48), ALU.mult))
                link(dve.tensor_reduce(tf[:, 48:96], grid(0, 48), AX_X, ALU.add))
                load = tt[:, 1, 0:48]
                slots = tt[:, 2, 0:48]
                link(dve.tensor_scalar(load, tf[:, 48:96], -1.0, None, ALU.add))
                link(dve.tensor_copy(tf[:, 96:144], load))
                for full in range(RING, E, RING):
                    link(dve.tensor_scalar(slots, load, float(full), -float(RING), ALU.is_ge, ALU.mult))
                    link(dve.tensor_tensor(tf[:, 96:144], tf[:, 96:144], slots, ALU.add))
                link(dve.tensor_scalar(tf[:, 96:144], tf[:, 96:144], float(EW), None, ALU.mult))
                dve.tensor_copy(tab[:, 48:144], tf[:, 48:144]).then_inc(s_tab, 1)

            def route_results():
                link(dve.tensor_scalar(tmp, startT, float(P), None, ALU.mult))
                link(dve.tensor_tensor(pos[:, :, :], pos[:, :, :], rows(tmp, J), ALU.add))
                for j in range(J):
                    pick(pos[:, j, :], j, yif[:, j, :])
                dve.tensor_copy(yidx[:, :, :], yif[:, :, :]).then_inc(s_yi, 1)

            def stat(col, src):
                link(dve.bn_stats(st[:, col % 2, :], src))
                dve.bn_aggr(mv[:, col, :], st[:, col % 2, :]).then_inc(s_stat, 1)

            for step in prog:
                kind = step[0]
                if kind == "a_stat":
                    j = step[1]
                    dve.wait_ge(s_c[j], 16)
                    link(dve.tensor_reduce(cmx[:, j:j + 1], crow[:, j, :], AX_X, ALU.max))
                    dve.tensor_scalar(ncm[:, j:j + 1], cmx[:, j:j + 1], -1.0, None, ALU.mult).then_inc(s_ncm, 1)
                    dve.wait_ge(s_x[j], 16)
                    stat(j, xr[:, j, :])
                elif kind == "a_prep":
                    j = step[1]
                    dve.wait_ge(s_rstd, STN[("a_stat", j)] + 1)
                    dve.wait_ge(s_stat, STN[("a_stat", j)] + 1)
                    dve.scalar_tensor_tensor(nmr[:, j:j + 1], mv[:, j, 0:1], -1.0, rstd[:, j:j + 1],
                                             ALU.mult, ALU.mult).then_inc(s_nmr, 1)
                elif kind == "a_kvs":
                    j = step[1]
                    dve.wait_ge(s_ek, j + 1)
                    link(dve.reciprocal(krec[:, j:j + 1], ksum[:, j:j + 1]))
                    dve.wait_ge(s_kvs, j + 1)
                    if j == 0:
                        dve.wait_ge(s_cst, 16)
                    if j >= 2:
                        dve.wait_ge(s_a, j - 1)
                    dve.scalar_tensor_tensor(kvm[:, j % 2, :], ps[:, 2 + j % 2, 0:P], krec[:, j:j + 1], blk8,
                                             ALU.mult, ALU.mult).then_inc(s_kvm, 1)
                elif kind == "a_out":
                    j = step[1]
                    dve.wait_ge(s_a, j + 1)
                    link(dve.reciprocal(srec, ps[:, 5, :]))
                    if j:
                        dve.wait_ge(s_x1, j)
                    dve.tensor_tensor(sout, ps[:, 4, :], srec, ALU.mult).then_inc(s_ac, 1)
                elif kind == "ln_stat":
                    _, layer, j = step
                    if layer == 1:
                        dve.wait_ge(s_x1, j + 1)
                    else:
                        dve.wait_ge(s_x2 if layer == 2 else s_x3, j + 1)
                    stat(J * layer + j, xr[:, j, :])
                elif kind == "ln_z":
                    _, layer, j = step
                    n = LNN[step]
                    col = J * layer + j
                    dve.wait_ge(s_stat, STN[("ln_stat", layer, j)] + 1)
                    dve.wait_ge(s_rstd, STN[("ln_stat", layer, j)] + 1)
                    if n >= 2:
                        old = [p for p in prog if p[0] == "ln_z"][n - 2]
                        dve.wait_ge(s_tr, TRN[("ln_t", *old[1:])] + 1)
                        if old[1] == 3:
                            dve.wait_ge(s_zd, 16 * (old[2] + 1))
                    dve.tensor_scalar(zrow[:, n % 2, :], xr[:, j, :], mv[:, col, 0:1], rstd[:, col:col + 1],
                                      ALU.subtract, ALU.mult).then_inc(s_z, 1)
                elif kind == "f_gu":
                    _, h, c = step
                    n = h * NF + c
                    m = P if c < NF - 1 else LASTF
                    dve.wait_ge(s_sil, n + 1)
                    if n == 0:
                        dve.wait_ge(s_ffw, 6 * 16)
                    dve.scalar_tensor_tensor(ha[0:m, n % 2, :], ps[0:m, 4 + n % 2, :], b1[0:m, NF + c:NF + c + 1],
                                             hs[0:m, n % 2, :], ALU.add, ALU.mult).then_inc(s_act, 1)
                elif kind == "f_out":
                    j = step[1]
                    dve.wait_ge(s_xb, j + 1)
                    dve.wait_ge(s_fo, j + 1)
                    dve.tensor_tensor(xr[:, j, :], ps[:, 6 + (j + 1) % 2, :], xr[:, j, :], ALU.add).then_inc(s_x2, 1)
                elif kind == "q":
                    _, q, g = step
                    dve.wait_ge(s_q, 4 * q + g + 1)
                    for t in range(3):
                        c = dve.tensor_copy(qT[32 * t:32 * t + 32, q % 2, :, 4 * g + 3, :],
                                            ps[HD:P, 4 + t // 2, 256 * (t % 2):256 * (t % 2) + 256]
                                            .rearrange("p (b s) -> p b s", b=4))
                    c.then_inc(s_qcv, 1)
                elif kind == "s":
                    n = step[1]
                    dve.wait_ge(s_s, n + 1)
                    if n >= 4:
                        dve.wait_ge(s_p, n - 3)
                    link(dve.tensor_reduce(smx[:, n % 4, :], ps[:, 2 + n % 2, :].rearrange("p (u s) -> p u s", u=4),
                                           AX_X, ALU.max))
                    dve.tensor_scalar(snm[:, n % 4, :], smx[:, n % 4, :], -SCALE, None, ALU.mult).then_inc(s_snm, 1)
                elif kind == "pn":
                    probs(step[1])
                elif kind == "pv":
                    n = step[1]
                    b, hf = divmod(n, 2)
                    j = b // 2
                    side = slice(S * (b % 2), S * (b % 2) + S)
                    dve.wait_ge(s_o, n + 1)
                    if j >= 2 and b % 2 == 0 and hf == 0:
                        dve.wait_ge(s_op, j - 1)
                    src = ps[:, 6, :].rearrange("p (g h q) -> p g h q", g=2, h=HG)
                    dst = oT[:, j % 2, 6 * hf:6 * hf + 6, side].rearrange("p (g t) q -> p g t q", g=2)
                    for g in range(2):
                        dve.tensor_copy(dst[0:HD, g, :, :], src[0:HD, g, 0:3, :])
                    for t in range(3):
                        c = dve.tensor_copy(dst[HD:P, :, t, :], src[32 * t:32 * t + 32, :, 3, :])
                    c.then_inc(s_oc, 1)
                elif kind == "op1":
                    j = step[1]
                    dve.wait_ge(s_op, j + 1)
                    dve.tensor_tensor(xr[:, j, :], ps[:, 7, :], xr[:, j, :], ALU.add).then_inc(s_x3, 1)
                elif kind == "gate":
                    j = step[1]
                    if j == 0:
                        dve.wait_ge(s_small, 32)
                        dve.wait_ge(s_tables, 16)
                        dve.wait_ge(s_ms, 3)
                    dve.wait_ge(s_ge, j + 1)
                    link(dve.tensor_scalar(gsc[:, 1, :], gsc[:, 0, :], 1.0, None, ALU.add))
                    link(dve.reciprocal(gsc[:, 2, :], gsc[:, 1, :]))
                    link(dve.tensor_tensor(gsc[:, 3, :], gsc[:, 2, :], gb[:, :], ALU.add))
                    link(dve.max(top8[:, :], gsc[:, 3, :]))
                    link(dve.max_index(idx8[:, :], top8[:, :], gsc[:, 3, :]))
                    link(dve.tensor_copy(idxf[:, :], idx8[:, :]))
                    link(dve.tensor_tensor(onehot[:, j, :, :],
                                           idxf[:, 0:TOPK].rearrange("p (k a) -> p k a", a=1).to_broadcast((P, TOPK, E)),
                                           iota16.rearrange("p (a e) -> p a e", a=1).to_broadcast((P, TOPK, E)),
                                           ALU.is_equal))
                    link(dve.tensor_reduce(mask[:, j, :], onehot[:, j, :, :].rearrange("p k e -> p e k"), AX_X, ALU.add))
                    dve.tensor_tensor(mcum[:, j + 1, :], mcum[:, j, :], mask[:, j, :], ALU.add).then_inc(s_mk, 1)
                    link(dve.tensor_reduce(wsum[:, :], top8[:, 0:TOPK], AX_X, ALU.add))
                    link(dve.tensor_scalar(wsum[:, :], wsum[:, :], 1e-20, None, ALU.add))
                    link(dve.reciprocal(wsum[:, :], wsum[:, :]))
                    link(dve.tensor_scalar(wtop[:, j, :], top8[:, 0:TOPK], wsum[:, 0:1], None, ALU.mult))
                elif kind == "place":
                    j = step[1]
                    dve.wait_ge(s_ps, j + 1)
                    dve.wait_ge(s_mk, j + 1)
                    link(dve.tensor_copy(pos[:, j, :], ps[:, 7, 0:E]))
                    link(dve.tensor_tensor(slot[:, :], pos[:, j, :], iota16c, ALU.add))
                    pick(slot[:, :], j, slotf[:, :])
                    dve.tensor_copy(sloti[:, j, :], slotf[:, :]).then_inc(s_sl, 1)
                elif kind == "route":
                    route(step[1])
                elif kind == "sh_gu":
                    j = step[1]
                    dve.wait_ge(s_hsil, j + 1)
                    if j >= 2:
                        dve.wait_ge(s_ht, j - 1)
                    dve.tensor_tensor(zg[:, j % 2, :], ps[:, 4 - 2 * (j % 2), I:2 * I], sg[:, j % 2, :],
                                      ALU.mult).then_inc(s_hz, 1)
                elif kind == "sh_d":
                    j = step[1]
                    dve.wait_ge(s_hd, j + 1)
                    dve.wait_ge(s_x3, j + 1)
                    dve.tensor_tensor(xr[:, j, :], ps[:, 5, :], xr[:, j, :], ALU.add).then_inc(s_x4, 1)

            def mul(i, par):
                dve.wait_ge(s_esil, i + 1)
                dve.tensor_tensor(zg[:, par, :], ps[:, 4 + par, I:2 * I], sg[:, par, :], ALU.mult).then_inc(s_ez, 1)

            def y_copy(i, par, wait_stored):
                dve.wait_ge(s_ed, i + 2)
                if wait_stored is not None:
                    dve.wait_ge(s_ys[par], wait_stored)
                dve.tensor_copy(yrow[:, par, :], ps[:, 6 + par, :]).then_inc(s_yc, 1)

            dve.wait_ge(s_tabl, 1)
            pairs = dve.value_load(tab[0:1, 193:194], min_val=16, max_val=TILES // 2)
            for i in range(3):
                mul(i, i % 2)
                if i:
                    y_copy(i - 1, (i - 1) % 2, None)
            with dve.Fori(1, 2 * pairs - 2, 2) as n:
                mul(n + 2, 1)
                y_copy(n + 1, 0, 8 * n + 8)
                mul(n + 3, 0)
                y_copy(n + 2, 1, 8 * n + 8)
            y_copy(2 * pairs, 0, pairs * 16)
            for m in range(J * TOPK):
                j, k = divmod(m, TOPK)
                dve.wait_ge(s_yg[m % NY], 16 * (m // NY + 1))
                if m:
                    dve.wait_ge(s_cmb, m)
                dve.scalar_tensor_tensor(xr[:, j, :], ygot[:, m % NY, :], wtop[:, j, k:k + 1], xr[:, j, :],
                                         ALU.mult, ALU.add).then_inc(s_cmb, 1)

        @block.tensor
        def _(pe):
            pe.wait_ge(s_cst, 16)

            def tbank(step):
                n = TRN[step]
                if n >= 2:
                    pe.wait_ge(s_trc, n - 1)
                return ps[:, n % 2, :]

            def transposes(bank, src, n):
                for c in range(n):
                    mm = pe.transpose(bank[:, c * P:(c + 1) * P], src[:, c * P:(c + 1) * P], ident)
                return mm

            def normed(layer, j):
                pe.wait_ge(s_trc, TRN[("ln_t", layer, j)] + 1)

            def dense(out, lhs, rhs, n):
                for k in range(n):
                    mm = pe.matmul(out, lhs(k), rhs(k), start=(k == 0), stop=(k == n - 1))
                return mm

            for step in prog:
                kind = step[0]
                if kind == "a_t":
                    j = step[1]
                    pe.wait_ge(s_ek, j + 1)
                    transposes(tbank(step), ek[:, j % 2, :], KC).then_inc(s_tr, 1)
                elif kind == "a_kvs":
                    j = step[1]
                    pe.wait_ge(s_trc, TRN[("a_t", j)] + 1)
                    pe.wait_ge(s_ct[j // 2], 16)
                    if j >= 2:
                        pe.wait_ge(s_kvm, j - 1)
                    dense(ps[:, 2 + j % 2, 0:P], lambda k: ekT[:, j % 2, k * P:(k + 1) * P],
                          lambda k: ctxT[:, k, j * P:(j + 1) * P], KC).then_inc(s_kvs, 1)
                elif kind == "a_out":
                    j = step[1]
                    pe.wait_ge(s_kvm, j + 1)
                    pe.wait_ge(s_eq, j + 1)
                    if j:
                        pe.wait_ge(s_ac, j)
                    pe.matmul(ps[:, 4, :], kvm[:, j % 2, :], eq[:, j % 2, :], start=True, stop=True)
                    pe.matmul(ps[:, 5, :], blk8, eq[:, j % 2, :], start=True, stop=True).then_inc(s_a, 1)
                elif kind == "kv":
                    unit = step[1]
                    n = KVN[step]
                    lat = unit[-1]
                    src = zT if lat else ctxT
                    js = range(4 * unit[2], 4 * unit[2] + 4) if unit[0] == "k" else (unit[1],)
                    if n >= 2:
                        pe.wait_ge(s_prc, n - 1)
                    if n == len(ctx_units):
                        pe.wait_ge(s_x2, J)
                    if lat:
                        for j in js:
                            normed(2, j)
                    else:
                        for j in js[::2]:
                            pe.wait_ge(s_ct[j // 2], 16)
                    if unit[0] == "k":
                        pe.wait_ge(s_wk, 16)
                        t, h = unit[1:3]
                        dense(ps[:, 6 + n % 2, :], lambda k: wk[:, k, t * P:(t + 1) * P],
                              lambda k: src[:, k, h * 512:(h + 1) * 512], KC).then_inc(s_pr, 1)
                    else:
                        pe.wait_ge(s_wv, 16)
                        j = unit[1]
                        dense(ps[:, 6 + n % 2, 0:G * HD], lambda k: src[:, k, j * P:(j + 1) * P],
                              lambda k: wv[:, k, :], KC).then_inc(s_pr, 1)
                elif kind == "ln_t":
                    n = LNN[("ln_z", *step[1:])]
                    pe.wait_ge(s_z, n + 1)
                    transposes(tbank(step), zrow[:, n % 2, :], KC).then_inc(s_tr, 1)
                elif kind == "f_in":
                    h = step[1]
                    for j in range(4 * h, 4 * h + 4):
                        normed(1, j)
                    if h == 0:
                        pe.wait_ge(s_ffw, 6 * 16)
                        pe.wait_ge(s_prc, len(ctx_units))
                    else:
                        pe.wait_ge(s_x2, 4)
                    dense(ps[:, 7, :], lambda k: u1[:, k, :], lambda k: zT[:, k, h * 512:(h + 1) * 512], KC)\
                        .then_inc(s_pt, 1)
                elif kind == "f_gu":
                    _, h, c = step
                    n = h * NF + c
                    m = P if c < NF - 1 else LASTF
                    pe.wait_ge(s_ptc, h + 1)
                    if n == 0:
                        pe.wait_ge(s_kvm, J)
                        pe.wait_ge(s_ac, J)
                    if n >= 2:
                        pe.wait_ge(s_act, n - 1)
                    pe.matmul(ps[0:m, 2 + n % 2, :], v1[:, c * P:c * P + m], pT, start=True, stop=True)
                    pe.matmul(ps[0:m, 4 + n % 2, :], v1[:, INTER + c * P:INTER + c * P + m], pT,
                              start=True, stop=True).then_inc(s_gu, 1)
                elif kind == "f_z":
                    _, h, c = step
                    n = h * NF + c
                    m = P if c < NF - 1 else LASTF
                    pe.wait_ge(s_act, n + 1)
                    mm = pe.matmul(ps[:, 6, :], u2[0:m, c, :], ha[0:m, n % 2, :], start=(c == 0), stop=(c == NF - 1))
                    if c == NF - 1:
                        mm.then_inc(s_oz, 1)
                elif kind == "f_out":
                    j = step[1]
                    pe.wait_ge(s_ozc, j // 4 + 1)
                    if j % 4 >= 2:
                        pe.wait_ge(s_x2, j - 1)
                    pe.matmul(ps[:, 6 + (j + 1) % 2, :], oz[:, (j % 4) * P:(j % 4 + 1) * P], v2,
                              start=True, stop=True).then_inc(s_fo, 1)
                elif kind == "q":
                    _, q, g = step
                    n = 4 * q + g
                    if n == 0:
                        pe.wait_ge(s_wq, 16)
                        pe.wait_ge(s_act, 2 * NF)
                    else:
                        pe.wait_ge(s_qca, n)
                        pe.wait_ge(s_qcv, n)
                    normed(2, 2 * q)
                    normed(2, 2 * q + 1)
                    for t in range(3):
                        mm = dense(ps[:, 4 + t // 2, 256 * (t % 2):256 * (t % 2) + 256],
                                   lambda k: wq[:, k, (3 * g + t) * P:(3 * g + t + 1) * P],
                                   lambda k: zT[:, k, 256 * q:256 * q + 256], KC)
                    mm.then_inc(s_q, 1)
                elif kind == "s":
                    n = step[1]
                    b, hf = divmod(n, 2)
                    q = b // 4
                    if n == 0:
                        pe.wait_ge(s_prc, len(ctx_units) + 14)
                    pe.wait_ge(s_qca, 4 * q + 2 * hf + 2)
                    pe.wait_ge(s_qcv, 4 * q + 2 * hf + 2)
                    if n >= 2:
                        pe.wait_ge(s_p, n - 1)
                    for u in range(4):
                        g = 2 * hf + u // 2
                        h0 = 4 * g + 2 * (u % 2)
                        mm = pe.matmul(ps[:, 2 + n % 2, u * P:(u + 1) * P],
                                       qT[0:HD, q % 2, b % 4, h0:h0 + 2, :].rearrange("p h s -> p (h s)"), kT[0:HD, g, b, :],
                                       start=True, stop=True)
                    mm.then_inc(s_s, 1)
                elif kind == "t":
                    n = step[1]
                    pe.wait_ge(s_pn, n + 1)
                    transposes(tbank(step), prob[:, n % 2, :, :].rearrange("p u s -> p (u s)"), 4).then_inc(s_tr, 1)
                elif kind == "pv":
                    n = step[1]
                    b, hf = divmod(n, 2)
                    pe.wait_ge(s_trc, TRN[("t", n)] + 1)
                    if n:
                        pe.wait_ge(s_oc, n)
                    for g in range(2):
                        c0 = HD * (2 * hf + g)
                        mm = pe.matmul(ps[0:HD, 6, 256 * g:256 * g + 256], v[:, b, c0:c0 + HD],
                                       probT[:, n % 2, 256 * g:256 * g + 256], start=True, stop=True)
                    mm.then_inc(s_o, 1)
                elif kind in ("op0", "op1"):
                    j = step[1]
                    if kind == "op0":
                        pe.wait_ge(s_oc, 4 * j + 4)
                        if j == 0:
                            pe.wait_ge(s_wo, 16)
                        else:
                            pe.wait_ge(s_x3, j)
                        if j >= 2:
                            pe.wait_ge(s_sl, j - 1)
                    for m in range(NQT // 2 * int(kind[2]), NQT // 2 * (int(kind[2]) + 1)):
                        mm = pe.matmul(ps[:, 7, :], oT[:, j % 2, m, :], wo[:, m, :], start=(m == 0), stop=(m == NQT - 1))
                    if kind == "op1":
                        mm.then_inc(s_op, 1)
                elif kind == "gate":
                    j = step[1]
                    normed(3, j)
                    pe.wait_ge(s_small, 32)
                    pe.wait_ge(s_x3, min(j + 2, J))
                    if j:
                        pe.wait_ge(s_sl, j)
                    dense(ps[:, 7, 0:E], lambda k: zT[:, k, j * P:(j + 1) * P], lambda k: gw[:, k, :], KC)\
                        .then_inc(s_g, 1)
                elif kind == "place":
                    j = step[1]
                    pe.wait_ge(s_mk, j + 1)
                    if j == 0:
                        pe.wait_ge(s_ms, 3)
                        pe.wait_ge(s_tables, 16)
                    pe.matmul(ps[:, 7, 0:E], tri, mask[:, j, :], start=True, stop=False)
                    pe.matmul(ps[:, 7, 0:E], ones, mcum[:, j, :], start=False, stop=True).then_inc(s_ps, 1)
                elif step == ("route", 0):
                    pe.wait_ge(s_sl, J)
                    pe.matmul(ps[:, 7, 0:E], ones, mcum[:, J, :], start=True, stop=True).then_inc(s_tot, 1)
                elif kind == "sh_gu":
                    j = step[1]
                    if j == 0:
                        pe.wait_ge(s_ws, 16)
                        pe.wait_ge(s_p, NU)
                        pe.wait_ge(s_qca, 4 * G)
                        pe.wait_ge(s_qcv, 4 * G)
                    if j >= 2:
                        pe.wait_ge(s_hz, j - 1)
                    normed(3, j)
                    dense(ps[:, 4 - 2 * (j % 2), :], lambda k: zT[:, k, j * P:(j + 1) * P],
                          lambda k: wsh[:, k * D:(k + 1) * D], KC).then_inc(s_hg, 1)
                elif kind == "sh_t":
                    j = step[1]
                    pe.wait_ge(s_hz, j + 1)
                    if j:
                        pe.wait_ge(s_htc, j)
                    transposes(ps[:, 3, :], zg[:, j % 2, :], I // P).then_inc(s_ht, 1)
                elif kind == "sh_d":
                    j = step[1]
                    pe.wait_ge(s_htc, j + 1)
                    if j:
                        pe.wait_ge(s_x4, j)
                    dense(ps[:, 5, :], lambda c: zgT[:, j % 2, c * P:(c + 1) * P],
                          lambda c: wsh[:, (KC + c) * D:(KC + c + 1) * D], I // P).then_inc(s_hd, 1)
                elif kind == "ids":
                    pe.wait_ge(s_idl, 16)
                    pe.wait_ge(s_trc, len(TRN))
                    pe.transpose(ps[:, 0, 0:P], idrow[:, :], ident).then_inc(s_idt, 1)

            def up(sem, value):
                if not isinstance(value, int) or value > 0:
                    pe.wait_ge(sem, value)

            def rows_in(i, par):
                pe.wait_ge(s_gx[par], i * 8 + (16 if par == 0 else 8))
                up(s_txc, i - 1)
                transposes(ps[:, par, :], xrow[:, par, :], KC).then_inc(s_tx, 1)

            def gate_up(i, par):
                load = pe.value_load(tab[0:1, bass.ds(i + 48, 1)], min_val=1, max_val=E)
                at = pe.value_load(tab[0:1, bass.ds(i + 96, 1)], min_val=0, max_val=(RING - 1) * EW)
                pe.wait_ge(s_w, load)
                pe.wait_ge(s_txc, i + 1)
                up(s_ez, i - 1)
                dense(ps[:, 4 + par, :], lambda k: xT[:, par, k * P:(k + 1) * P],
                      lambda k: ering[:, bass.ds(at + k * D, D)], KC).then_inc(s_eg, 1)

            def act_in(i, par, copied):
                pe.wait_ge(s_ez, i + 1)
                up(s_tzc, copied)
                transposes(ps[:, 2 + par, :], zg[:, par, :], I // P).then_inc(s_tz, 1)

            def down(i, par, copied):
                at = pe.value_load(tab[0:1, bass.ds(i + 96, 1)], min_val=0, max_val=(RING - 1) * EW)
                pe.wait_ge(s_tzc, i + 1)
                up(s_yc, copied)
                dense(ps[:, 6 + par, :], lambda c: zgT[:, par, c * P:(c + 1) * P],
                      lambda c: ering[:, bass.ds(at + (KC + c) * D, D)], I // P).then_inc(s_ed, 1)

            def pe_step(i, par):
                rows_in(i + 1, 1 - par)
                if not isinstance(i, int) or i:
                    act_in(i - 1, 1 - par, i - 2)
                gate_up(i, par)
                if not isinstance(i, int) or i:
                    down(i - 1, 1 - par, i - 2)

            pe.wait_ge(s_tabl, 1)
            pe.wait_ge(s_tab, 1)
            pe.wait_ge(s_ids, 1)
            pe.wait_ge(s_x4, J)
            pe.sem_inc(s_ed, 1)
            pairs = pe.value_load(tab[0:1, 193:194], min_val=16, max_val=TILES // 2)
            rows_in(0, 0)
            for i in range(3):
                pe_step(i, i % 2)
            with pe.Fori(1, 2 * pairs - 2, 2) as n:
                pe_step(n + 2, 1)
                pe_step(n + 3, 0)
            act_in(2 * pairs, 0, 2 * pairs)
            down(2 * pairs, 0, 2 * pairs)


_INS = ["x", "ctx", "ctxT", "consts", "U1", "V1", "U2", "V2", "b1", "b2", "Wq", "Wk", "Wv", "Wo",
        "gate", "bias", "experts", "shared"]


def kernel(**inputs):
    import numpy as np
    import concourse.bacc as bacc
    from concourse import mybir as _mybir
    from concourse.bass_utils import run_bass_kernel_spmd as run

    a = {k: np.asarray(v) for k, v in inputs.items()}
    f = np.float32

    def chunks(w):
        n = w.shape[0] // P
        return np.ascontiguousarray(w.reshape(n, P, -1).transpose(1, 0, 2).reshape(P, -1))

    order = []
    for g in range(G):
        for t in range(3):
            order += [(g * HG + t) * HD + d for d in range(HD)]
            order += [(g * HG + 3) * HD + 32 * t + d for d in range(32)]
    korder = []
    for t in range(3):
        korder += [t * HD + d for d in range(HD)] + [3 * HD + 32 * t + d for d in range(32)]

    ctx = a["ctx_4096"].reshape(T, D)
    u2 = np.zeros((NF * P, RANK), f)
    u2[:INTER] = a["L0_ffn_U2"]
    b1 = np.zeros((2, NF * P), f)
    b1[:, :INTER] = a["L0_ffn_b1"].reshape(2, INTER)
    i = np.arange(P)
    cst = np.zeros((P, 4 * P + 176), f)
    cst[:, 0:P] = np.eye(P)
    cst[:, P:2 * P] = (i[:, None] // DH == i[None, :] // DH)
    cst[:, 2 * P:3 * P] = (i[:, None] < i[None, :])
    cst[:, 3 * P:4 * P] = 1
    c0 = 4 * P
    cst[:, c0:c0 + 16] = np.arange(E)
    cst[:, c0 + 16:c0 + 32] = 8 * np.arange(E)
    cst[:, c0 + 32:c0 + 48] = T * np.arange(E)
    cst[:, c0 + 48:c0 + 56] = P * np.arange(8)
    cst[:, c0 + 56:c0 + 72] = (np.arange(E) % RING) * EW
    cst[:, c0 + 72:c0 + 120] = np.arange(48)
    cst[:, c0 + 120:c0 + 144] = 2 * np.arange(1, 25)
    cst[:, c0 + 144:c0 + 152] = P * np.arange(J)[None, :] + i[:, None]

    def expert(g, u, d):
        gu = np.concatenate([g.T.reshape(KC, P, I), u.T.reshape(KC, P, I)], axis=2)
        return np.concatenate([gu.transpose(1, 0, 2).reshape(P, -1), chunks(d.T)], axis=1)

    host = {
        "x": a["x"].reshape(T, D), "ctx": ctx,
        "ctxT": ctx.T.reshape(KC, P, T).transpose(1, 0, 2),
        "consts": cst,
        "U1": chunks(a["L0_ffn_U1"]), "V1": a["L0_ffn_V1"], "U2": chunks(u2), "V2": a["L0_ffn_V2"],
        "b1": b1.reshape(2 * NF, P).T, "b2": a["L0_ffn_b2"].reshape(1, D),
        "Wq": chunks(a["L1_xattn_Wq"][order].T), "Wk": chunks(a["L1_xattn_Wk"][korder].T),
        "Wv": chunks(a["L1_xattn_Wv"].T), "Wo": chunks(a["L1_xattn_Wo"].T[order]),
        "gate": chunks(a["L1_ffn_gate_w"].T), "bias": a["L1_ffn_bias"].reshape(1, E),
        "experts": np.stack([expert(a["L1_ffn_Wg"][e], a["L1_ffn_Wu"][e], a["L1_ffn_Wd"][e]) for e in range(E)]),
        "shared": expert(a["L1_ffn_Sg"], a["L1_ffn_Su"], a["L1_ffn_Sd"]),
    }
    nc = bacc.Bacc("TRN2", target_bir_lowering=False, num_devices=1)
    arrays, args = {}, []
    for name in _INS:
        arr = np.ascontiguousarray(host[name])
        arrays[f"in_{name}"] = arr
        args.append(nc.dram_tensor(f"in_{name}", arr.shape, _mybir.dt.from_np(arr.dtype), kind="ExternalInput").ap())
    out = nc.dram_tensor("out", (T, D), F32, kind="ExternalOutput").ap()
    build(nc, *args, out)
    r = run(nc, [arrays], core_ids=[0])
    return r.results[0]["out"].reshape(B, S, D)
```

```python
from contextlib import ExitStack

import concourse.bass as bass
from concourse import mybir

F32 = mybir.dt.float32
I32 = mybir.dt.int32
U32 = mybir.dt.uint32
ALU = mybir.AluOpType
ACT = mybir.ActivationFunctionType
AX_X = mybir.AxisListType.X

P = 128
B, S, D = 16, 64, 512
T = B * S
J = T // P
KC = D // P
DH = 8
RANK, INTER = 128, 1376
NF = -(-INTER // P)
LASTF = INTER - (NF - 1) * P
G, HG, HD = 4, 4, 96
NQT = G * 3
E, I, TOPK = 16, 256, 4
EW = (KC + I // P) * D
TILES = T * TOPK // P + E - 1
RING = 4
EPS = 1e-5
SCALE = float(HD) ** -0.5


def build(nc, x_d, ctx_d, ctxT_d, cst_d, u1_d, v1_d, u2_d, v2_d, b1_d, b2_d,
          wq_d, wk_d, wv_d, wo_d, gw_d, gb_d, we_d, ws_d, free_d, out_d):
    z_d = nc.dram_tensor("z_rows", (T + P, D), F32, kind="Internal").ap()
    id_d = nc.dram_tensor("slots", (P, 2 * P), F32, kind="Internal").ap()

    with ExitStack() as stack:
        def sb(name, shape, dt=F32):
            return stack.enter_context(nc.sbuf_tensor(name, shape, dt))

        def sem(name):
            return stack.enter_context(nc.semaphore(name))

        xr = sb("xr", [P, J, D])
        cst = sb("cst", [P, 4 * P + 176])
        zT = sb("zT", [P, KC, T])
        r1 = sb("r1", [P, 8192])
        r3 = sb("r3", [P, 6144])
        r4 = sb("r4", [P, 3072])
        rq = sb("rq", [P, 8192])
        kv = sb("kv", [P, 14336])
        zrow = sb("zrow", [P, 2, D])

        ident, blk8, tri, ones = (cst[:, i * P:(i + 1) * P] for i in range(4))
        c0 = 4 * P
        iota16 = cst[:, c0:c0 + 16]
        iota16c = cst[:, c0 + 32:c0 + 48]
        m128 = cst[:, c0 + 48:c0 + 56]
        ringo = cst[:, c0 + 56:c0 + 72]
        iota48 = cst[:, c0 + 72:c0 + 120]
        even24 = cst[:, c0 + 120:c0 + 144]
        tokid = cst[:, c0 + 144:c0 + 153]
        ctxT = r1[:, 0:4096].rearrange("p (k t) -> p k t", k=KC)
        crow = r1[:, 4096:8192].rearrange("p (j d) -> p j d", j=J)
        wq = r1[:, 0:6144].rearrange("p (k m) -> p k m", k=KC)
        prob = r1[:, 6144:7168].rearrange("p (n u s) -> p n u s", n=2, u=4)
        probT = r1[:, 7168:8192].rearrange("p (n c) -> p n c", n=2)
        u1 = r3[:, 0:512].rearrange("p (k r) -> p k r", k=KC)
        v1 = r3[:, 512:512 + 2 * INTER]
        u2 = r3[:, 3264:3264 + NF * RANK].rearrange("p (c r) -> p c r", c=NF)
        v2 = r3[:, 4672:5184]
        b2 = r3[:, 5184:5696]
        b1 = r3[:, 5696:5696 + 2 * NF]
        wo = r3[:, 0:6144].rearrange("p (m d) -> p m d", m=NQT)
        ek = r4[:, 0:1024].rearrange("p (n d) -> p n d", n=2)
        eq = r4[:, 1024:2048].rearrange("p (n d) -> p n d", n=2)
        ekT = r4[:, 2048:3072].rearrange("p (n c) -> p n c", n=2)
        oT = r4[:, 0:3072].rearrange("p (n m t) -> p n m t", n=2, m=NQT)
        qT = rq[:, :].rearrange("p (n b h s) -> p n b h s", n=2, b=4, h=G * HG)
        hs = rq[:, 0:1024].rearrange("p (n t) -> p n t", n=2)
        ha = rq[:, 1024:2048].rearrange("p (n t) -> p n t", n=2)
        pT = rq[:, 2048:2560]
        oz = rq[:, 2560:3072]
        srec = rq[:, 3072:3584]
        sout = rq[:, 3584:4096]
        wk = rq[:, 4096:4096 + KC * G * HD].rearrange("p (k m) -> p k m", k=KC)
        wv = rq[:, 5632:5632 + KC * G * HD].rearrange("p (k m) -> p k m", k=KC)
        kT = kv[:, 0:8192].rearrange("p (g b s) -> p g b s", g=G, b=B)
        v = kv[:, 8192:14336].rearrange("p (b c) -> p b c", b=B)
        ering = kv[:, 0:RING * EW]
        wsh = r1[:, 0:EW]
        zs = r1[:, 3072:3072 + J * I].rearrange("p (j i) -> p j i", j=J)
        xrow = rq[:, 0:1024].rearrange("p (n d) -> p n d", n=2)
        xT = rq[:, 1024:2048].rearrange("p (n c) -> p n c", n=2)
        sg = rq[:, 2048:2560].rearrange("p (n i) -> p n i", n=2)
        zg = rq[:, 2560:3072].rearrange("p (n i) -> p n i", n=2)
        zgT = rq[:, 3072:3584].rearrange("p (n i) -> p n i", n=2)
        yrow = rq[:, 3584:4608].rearrange("p (n d) -> p n d", n=2)
        kvm = sb("kvm", [P, 2, P])
        gw = sb("gw", [P, KC, E])
        gb = sb("gb", [P, E])
        zero = sb("zero", [P, P])
        half = sb("half", [P, 1])
        st = sb("st", [P, 2, 6])
        mv = sb("mv", [P, 4 * J, 2])
        ve = sb("ve", [P, 4 * J])
        rstd = sb("rstd", [P, 4 * J])
        nmr = sb("nmr", [P, J])
        cmx = sb("cmx", [P, J])
        ncm = sb("ncm", [P, J])
        ksum = sb("ksum", [P, J])
        krec = sb("krec", [P, J])
        smx = sb("smx", [P, 4, 4])
        snm = sb("snm", [P, 4, 4])
        ssum = sb("ssum", [P, 4, 4])
        srs = sb("srs", [P, 4, 4])
        gsc = sb("gsc", [P, 4, E])
        top8 = sb("top8", [P, 8])
        idx8 = sb("idx8", [P, 8], U32)
        idxf = sb("idxf", [P, 8])
        onehot = sb("onehot", [P, J, TOPK, E])
        mask = sb("mask", [P, J, E])
        mcum = sb("mcum", [P, J + 1, E])
        pos = sb("pos", [P, E])
        slot = sb("slot", [P, E])
        ohs = sb("ohs", [P, TOPK, E])
        slotf = sb("slotf", [P, TOPK])
        sloti = sb("sloti", [P, J, TOPK], I32)
        wsum = sb("wsum", [P, 1])
        tokw = sb("tokw", [P, J, TOPK, 2])
        tb = sb("tb", [P, 12, E])
        tt = r4[:, 0:3 * 48 * E].rearrange("p (n c) -> p n c", n=3)
        tf = sb("tf", [P, 3 * 48 + 3 * E + 3])
        tab = sb("tab", [P, 3 * 48 + 3 * E + 3], I32)
        idrow = sb("idrow", [P, P, 2])
        ids = sb("ids", [P, P + 1], I32)
        wts = sb("wts", [P, P + 1])
        gidx = sb("gidx", [P, 2], I32)
        sidx = sb("sidx", [P, 2], I32)

        ps = stack.enter_context(nc.psum_tensor("ps", [P, 8, 512], F32))

        nE = tb[:, 0, :]

        s_cst = sem("identity_and_blocks_loaded")
        s_tables = sem("count_constants_loaded")
        s_c = [sem(f"context_rows_loaded{j}") for j in range(J)]
        s_x = [sem(f"x_rows_loaded{j}") for j in range(J)]
        s_wk = sem("wk_loaded")
        s_wv = sem("wv_loaded")
        s_ct = [sem(f"ctxT_loaded{h}") for h in range(J // 2)]
        s_ffw = sem("ffn_weights_loaded")
        s_small = sem("gate_weights_loaded")
        s_wq = sem("wq_loaded")
        s_wo = sem("wo_loaded")
        s_ws = sem("shared_weights_loaded")
        s_ms = sem("memsets_done")
        s_idz = sem("slots_freed")
        s_pad = sem("free_rows_zeroed")
        chain_v = sem("vector_chain")
        chain_p = sem("pool_chain")
        s_stat = sem("stats_done")
        s_rstd = sem("rstd_done")
        s_ncm = sem("ctx_negmax_done")
        s_nmr = sem("x_shift_done")
        s_ek = sem("exp_k_done")
        s_eq = sem("exp_q_done")
        s_tr = sem("transposes_done")
        s_trc = sem("transposes_copied")
        s_kvs = sem("kvs_done")
        s_kvm = sem("kvs_masked")
        s_a = sem("first_attention_done")
        s_ac = sem("first_attention_scaled")
        s_x1 = sem("x1_done")
        s_z = sem("z_done")
        s_xb = sem("x1_plus_b2_done")
        s_pr = sem("kv_projection_done")
        s_prc = sem("kv_projection_copied")
        s_pt = sem("rank_in_done")
        s_ptc = sem("rank_in_copied")
        s_gu = sem("ffn_gate_up_done")
        s_sil = sem("ffn_silu_done")
        s_act = sem("ffn_act_done")
        s_oz = sem("rank_out_done")
        s_ozc = sem("rank_out_copied")
        s_fo = sem("ffn_rows_done")
        s_x2 = sem("x2_done")
        s_q = sem("q_done")
        s_qca = sem("q_copied_act")
        s_qcv = sem("q_copied_dve")
        s_s = sem("scores_done")
        s_snm = sem("score_negmax_done")
        s_p = sem("exp_done")
        s_pn = sem("probs_done")
        s_o = sem("pv_done")
        s_oc = sem("pv_copied")
        s_op = sem("o_projection_done")
        s_x3 = sem("x3_done")
        s_zd = sem("z_rows_stored")
        s_mk = sem("expert_mask_done")
        s_free = sem("free_column_done")
        s_sl = sem("slots_done")
        s_sc = [sem(f"ids_scattered{k}") for k in range(TOPK)]
        s_tabl = sem("load_table_done")
        s_tabc = sem("tile_columns_done")
        s_tab = sem("tile_weights_done")
        s_idl = sem("slot_tokens_loaded")
        s_idt = sem("slot_tokens_transposed")
        s_ids = sem("slot_tokens_ready")
        s_hg = sem("shared_gate_up_done")
        s_hsil = sem("shared_silu_done")
        s_hz = sem("shared_act_done")
        s_ht = sem("shared_act_transposed")
        s_htc = sem("shared_act_copied")
        s_hd = sem("shared_down_done")
        s_x4 = sem("x4_done")
        s_wdma = [sem(f"expert_weights_dma{i}") for i in range(2)]
        s_w = sem("expert_weights_ready")
        s_gi = sem("gather_index_ready")
        s_giw = sem("pool_waits_passed")
        s_gx = [sem(f"rows_gathered{i}") for i in range(2)]
        s_tx = sem("rows_transposed")
        s_txc = sem("rows_copied")
        s_eg = sem("expert_gate_up_done")
        s_esil = sem("expert_silu_done")
        s_ez = sem("expert_act_done")
        s_tz = sem("act_transposed")
        s_tzc = sem("act_copied")
        s_ed = sem("expert_down_done")
        s_yc = sem("expert_rows_copied")
        s_si = sem("scatter_index_ready")
        s_ys = sem("expert_rows_added")
        s_out = sem("output_started")

        ctx_units = []
        for h in range(2):
            ctx_units += [("v", j, 0) for j in range(4 * h, 4 * h + 4)]
            ctx_units += [("k", t, h, 0) for t in range(3)]
        lat_units = []
        for h in range(2):
            lat_units.append([("k", t, h, 1) for t in range(3)] + [("v", j, 1) for j in range(4 * h, 4 * h + 4)])

        prog = []
        fill = list(ctx_units)
        prog += [("a_stat", 0), ("a_stat", 1)]
        per_step = (1, 2, 1, 2, 2, 2, 1, 2, 1, 0)
        prog.append(("a_prep", 0))
        for s in range(J + 2):
            if s < J:
                prog.append(("a_t", s))
            if 2 <= s:
                prog.append(("a_out", s - 2))
                prog.append(("x1", s - 2))
            if s == J + 1:
                prog.append(("f_in", 0))
            if s + 1 < J:
                prog.append(("a_prep", s + 1))
            if 1 <= s <= J:
                prog.append(("a_q", s - 1))
            if per_step[s]:
                prog.append(("kv", fill.pop(0)))
            if 1 <= s <= J:
                prog.append(("a_kvs", s - 1))
            if 4 <= s:
                prog.append(("ln_z", 1, s - 4))
            if s + 2 < J:
                prog.append(("a_stat", s + 2))
            if 3 <= s:
                prog.append(("ln_stat", 1, s - 3))
            if per_step[s] > 1:
                prog.append(("kv", fill.pop(0)))
            if 4 <= s:
                prog.append(("ln_t", 1, s - 4))
        for h in range(2):
            beside = {0: [(1, 6), (1, 7)], 1: [(2, j) for j in range(4)]}[h]
            for c in range(NF):
                prog.append(("f_gu", h, c))
                if h == 1 and c < 2:
                    prog += [("f_out", j) for j in ((1, 2), (3,))[c]]
                if c:
                    prog.append(("f_z", h, c - 1))
                i = c // 2
                if c % 2 == 0 and i < len(beside):
                    if beside[i] != (1, 6):
                        prog.append(("ln_stat", *beside[i]))
                if c % 2 == 1 and i < len(beside):
                    prog.append(("ln_z", *beside[i]))
                if c % 2 == 0 and 1 <= i <= len(beside):
                    prog.append(("ln_t", *beside[i - 1]))
            prog += [("f_z", h, NF - 1), ("f_oz", h)]
            if h == 0:
                prog.append(("f_in", 1))
            for j in (range(1), range(4, 8))[h]:
                prog.append(("f_out", j))
        for i, u in enumerate(lat_units[0]):
            if i < 4:
                prog.append(("ln_stat", 2, 4 + i))
            prog.append(("kv", u))
            if i < 4:
                prog.append(("ln_z", 2, 4 + i))
            if 1 <= i < 5:
                prog.append(("ln_t", 2, 3 + i))
        for i, u in enumerate(lat_units[1]):
            prog.append(("kv", u))
            if i in (1, 3, 5, 6):
                prog.append(("q", 0, (1, 3, 5, 6).index(i)))
        NU = 2 * B
        WAY = {False: [(7, 0, "op0"), (9, 0, "op1"), (9, 1, "ln_stat"), (10, 1, "ln_z"), (11, 2, "ln_t"),
                       (12, 1, "gate"), (13, 1, "place")],
               True: [(6, 0, "op0"), (7, 0, "op1"), (7, 1, "ln_stat"), (8, 1, "ln_z"), (9, 2, "ln_t"),
                      (9, 1, "gate"), (10, 1, "place")]}

        def way(n, place):
            for j in range(J):
                for off, at, what in WAY[j >= 5]:
                    if at == place and n == 4 * j + off:
                        prog.append((what, 3, j) if what[:3] == "ln_" else (what, j))

        BESIDE = {25: (0, 1), 29: (2, 3)}
        for n in range(NU + 1):
            if n < NU:
                prog.append(("s", n))
            for j in BESIDE.get(n, ()):
                prog.append(("sh_gu", j))
            if n < NU:
                prog.append(("pn", n))
            q, r = n // 8, n % 8
            if q < 3 and r % 2 == 0:
                prog.append(("q", q + 1, r // 2))
            way(n, 0)
            if 1 <= n <= NU:
                prog.append(("t", n - 1))
            way(n, 2)
            if 2 <= n <= NU + 1:
                prog.append(("pv", n - 2))
            way(n, 1)
        prog += [("pv", NU - 1), ("ln_t", 3, J - 2), ("op0", J - 1), ("op1", J - 1), ("ln_stat", 3, J - 1),
                 ("gate", J - 2), ("sh_t", 0), ("ln_z", 3, J - 1), ("sh_gu", 4), ("ln_t", 3, J - 1),
                 ("sh_d", 0), ("place", J - 2), ("sh_t", 1), ("gate", J - 1), ("sh_gu", 5), ("sh_d", 1),
                 ("place", J - 1), ("sh_t", 2), ("count",), ("route", 0), ("sh_gu", 6), ("route", 1), ("sh_t", 3),
                 ("sh_d", 2), ("sh_d", 3), ("sh_gu", 7), ("ids",), ("sh_t", 4), ("sh_t", 5), ("sh_d", 4),
                 ("route", 2), ("sh_t", 6), ("sh_d", 5), ("sh_t", 7), ("sh_d", 6), ("sh_d", 7)]

        def order(kinds):
            return {step: i for i, step in enumerate(p for p in prog if p[0] in kinds)}

        TRN = order(("a_t", "ln_t", "t", "gate", "place", "count"))
        KVN = order(("kv",))
        LNN = order(("ln_z",))
        STN = order(("a_stat", "ln_stat"))
        block = stack.enter_context(nc.Block())

        def halves(unit):
            return slice(S * unit[-1], S * unit[-1] + S)

        def shared_down(j):
            return ps[:, (6 if j < J - 2 else 4) + j % 2, :]

        @block.sync
        def _(sp):
            sp.dma_start(crow[:, 0, :], ctx_d[0:P, :]).then_inc(s_c[0], 16)
            sp.dma_start(cst[:, 0:2 * P], cst_d[:, 0:2 * P]).then_inc(s_cst, 16)
            for j in range(J):
                if j:
                    sp.dma_start(crow[:, j, :], ctx_d[j * P:(j + 1) * P, :]).then_inc(s_c[j], 16)
                sp.dma_start(xr[:, j, :], x_d[j * P:(j + 1) * P, :]).then_inc(s_x[j], 16)
                if j in (2, 4):
                    h = j // 2 + 1
                    sp.dma_start(ctxT[:, :, h * 256:(h + 1) * 256], ctxT_d[:, :, h * 256:(h + 1) * 256]).then_inc(s_ct[h], 16)
            sp.dma_start(u1, u1_d.rearrange("p (k r) -> p k r", k=KC)).then_inc(s_ffw, 16)
            sp.dma_start(v1, v1_d).then_inc(s_ffw, 16)
            sp.dma_start(u2, u2_d.rearrange("p (c r) -> p c r", c=NF)).then_inc(s_ffw, 16)
            sp.dma_start(v2, v2_d).then_inc(s_ffw, 16)
            sp.dma_start(b1, b1_d).then_inc(s_ffw, 16)
            sp.dma_start(b2, b2_d.to_broadcast((P, D))).then_inc(s_ffw, 16)
            sp.dma_start(gw[:, :, :], gw_d.rearrange("p (k e) -> p k e", k=KC)).then_inc(s_small, 16)
            sp.dma_start(gb[:, :], gb_d.to_broadcast((P, E))).then_inc(s_small, 16)
            sp.dma_start(cst[:, 2 * P:], cst_d[:, 2 * P:]).then_inc(s_tables, 16)
            sp.wait_ge(s_ms, 2)
            sp.dma_start(id_d, free_d).then_inc(s_idz, 16)
            for rows in (z_d, out_d):
                sp.dma_start(rows[T:T + P, :].rearrange("p (a c) -> p a c", c=P),
                             zero[:, :].rearrange("p (a c) -> p a c", a=1).to_broadcast((P, D // P, P)))\
                    .then_inc(s_pad, 16)
            sp.wait_ge(s_a, J)
            sp.wait_ge(s_ek, J)
            sp.wait_ge(s_ncm, J)
            sp.wait_ge(s_pr, len(ctx_units))
            sp.dma_start(wq, wq_d.rearrange("p (k m) -> p k m", k=KC)).then_inc(s_wq, 16)
            sp.wait_ge(s_fo, J)
            sp.wait_ge(s_xb, J)
            sp.wait_ge(s_act, 2 * NF)
            sp.dma_start(wo, wo_d.rearrange("p (m d) -> p m d", m=NQT)).then_inc(s_wo, 16)
            for j in range(J):
                if j == 3:
                    sp.wait_ge(s_q, 4 * G)
                    sp.dma_start(wsh, ws_d).then_inc(s_ws, 16)
                sp.wait_ge(s_z, LNN[("ln_z", 3, j)] + 1)
                sp.dma_start(z_d[j * P:(j + 1) * P, :], zrow[:, LNN[("ln_z", 3, j)] % 2, :]).then_inc(s_zd, 16)
                sp.wait_ge(s_zd, 16 * (j + 1))
            sp.wait_ge(s_tabl, 1)
            sp.wait_ge(s_o, NU)
            loads = sp.value_load(tab[0:1, 192:193], min_val=TOPK, max_val=E)
            first = sp.value_load(tab[0:1, 144:145], min_val=0, max_val=E - 1)
            sp.dma_start(ering[:, 0:EW], we_d[bass.ds(first, 1), :, :].rearrange("a p n -> (a p) n")).then_inc(s_wdma[0], 16)
            sp.wait_ge(s_wdma[0], 16)
            sp.sem_inc(s_w, 1)
            second = sp.value_load(tab[0:1, 145:146], min_val=0, max_val=E - 1)
            sp.dma_start(ering[:, EW:2 * EW], we_d[bass.ds(second, 1), :, :].rearrange("a p n -> (a p) n")).then_inc(s_wdma[1], 16)
            sp.wait_ge(s_wdma[1], 16)
            sp.sem_inc(s_w, 1)
            for j in range(J - 3, J):
                sp.wait_ge(s_x4, j + 1)
                sp.dma_start(out_d[j * P:(j + 1) * P, :], xr[:, j, :]).then_inc(s_out, 16)
            with sp.Fori(2, loads) as o:
                expert = sp.value_load(tab[0:1, bass.ds(o + 144, 1)], min_val=0, max_val=E - 1)
                free = sp.value_load(tab[0:1, bass.ds(o + 160, 1)], min_val=0, max_val=TILES)
                at = sp.value_load(tab[0:1, bass.ds(o + 176, 1)], min_val=0, max_val=(RING - 1) * EW)
                sp.wait_ge(s_ed, free + 1)
                sp.dma_start(ering[:, bass.ds(at, EW)],
                             we_d[bass.ds(expert, 1), :, :].rearrange("a p n -> (a p) n")).then_inc(s_wdma[1], 16)
                sp.wait_ge(s_wdma[1], 16 * o)
                sp.sem_inc(s_w, 1)

        @block.gpsimd
        def _(pool):
            def link(ins, n=[0]):
                n[0] += 1
                ins.then_inc(chain_p, 1)
                pool.wait_ge(chain_p, n[0])

            pool.memset(half[:, :], -0.5).then_inc(s_ms, 1)
            pool.memset(zero[:, :], 0.0).then_inc(s_ms, 1)
            pool.memset(mcum[:, 0, :], 0.0).then_inc(s_ms, 1)
            pool.wait_ge(s_ms, 1)
            stats = [0]

            def root(col):
                stats[0] += 1
                pool.wait_ge(s_stat, stats[0])
                link(pool.tensor_scalar(ve[:, col:col + 1], mv[:, col, 1:2], EPS, None, ALU.add))
                pool.tensor_tensor(rstd[:, col:col + 1], ve[:, col:col + 1], half[:, :], ALU.pow).then_inc(s_rstd, 1)

            for step in prog:
                if step[0] == "a_stat":
                    root(step[1])
                elif step[0] == "x1":
                    j = step[1]
                    pool.wait_ge(s_ac, j + 1)
                    pool.tensor_tensor(xr[:, j, :], xr[:, j, :], sout, ALU.add).then_inc(s_x1, 1)
                elif step[0] == "ln_stat":
                    root(J * step[1] + step[2])
                elif step[0] == "ln_z" and step[1] == 1:
                    j = step[2]
                    if j == 0:
                        pool.wait_ge(s_ffw, 6 * 16)
                    pool.wait_ge(s_z, LNN[step] + 1)
                    pool.tensor_tensor(xr[:, j, :], xr[:, j, :], b2, ALU.add).then_inc(s_xb, 1)
                elif step[0] == "place":
                    j = step[1]
                    pool.wait_ge(s_sl, j + 1)
                    pool.wait_ge(s_idz, 16)
                    for k in range(TOPK):
                        if j:
                            pool.wait_ge(s_sc[k], 16 * j)
                        pool.indirect_dma_start(
                            out=id_d.rearrange("a (b c) -> (a b) c", c=2),
                            out_offset=bass.IndirectOffsetOnAxis(ap=sloti[:, j, k:k + 1], axis=0),
                            in_=tokw[:, j, k, :], in_offset=None).then_inc(s_sc[k], 16)
            for k in range(TOPK):
                pool.wait_ge(s_sc[k], 16 * J)
            pool.dma_start(idrow[:, :, :].rearrange("p a c -> p (a c)"), id_d).then_inc(s_idl, 16)
            pool.wait_ge(s_tabl, 1)
            pool.wait_ge(s_tabc, 1)
            pool.wait_ge(s_ids, 1)
            pool.wait_ge(s_free, 1)
            pool.wait_ge(s_zd, 16 * J)
            pool.wait_ge(s_pad, 2 * 16)

            def gather(i, par, wait_rows, n):
                col = pool.value_load(tab[0:1, bass.ds(i, 1)], min_val=0, max_val=P)
                if wait_rows is not None:
                    pool.wait_ge(s_tx, wait_rows)
                    pool.wait_ge(s_gx[par], n * 16)
                pool.tensor_copy(gidx[:, par:par + 1], ids[:, bass.ds(col, 1)]).then_inc(s_gi, 1)
                pool.wait_ge(s_gi, i + 1)
                pool.sem_inc(s_giw, 1)
                pool.indirect_dma_start(out=xrow[:, par, :], out_offset=None, in_=z_d,
                                        in_offset=bass.IndirectOffsetOnAxis(ap=gidx[:, par:par + 1], axis=0),
                                        ).then_inc(s_gx[par], 16)

            def add_rows(i, par):
                col = pool.value_load(tab[0:1, bass.ds(i, 1)], min_val=0, max_val=P)
                if not isinstance(i, int) or i:
                    pool.wait_ge(s_ys, 16 * i)
                pool.tensor_copy(sidx[:, par:par + 1], ids[:, bass.ds(col, 1)]).then_inc(s_si, 1)
                pool.wait_ge(s_si, i + 1)
                pool.wait_ge(s_yc, i + 1)
                pool.sem_inc(s_giw, 1)
                pool.indirect_dma_start(out=out_d, in_=yrow[:, par, :], in_offset=None,
                                        out_offset=bass.IndirectOffsetOnAxis(ap=sidx[:, par:par + 1], axis=0),
                                        compute_op=ALU.add).then_inc(s_ys, 16)

            gather(0, 0, None, 0)
            gather(1, 1, None, 0)
            pairs = pool.value_load(tab[0:1, 193:194], min_val=16, max_val=TILES // 2)
            last = pool.value_load(tab[0:1, 194:195], min_val=30, max_val=TILES - 3)
            gather(2, 0, 1, 1)
            gather(3, 1, 2, 1)
            pool.wait_ge(s_out, 16 * J)
            gather(4, 0, 3, 2)
            add_rows(0, 0)
            gather(5, 1, 4, 2)
            add_rows(1, 1)
            with pool.Fori(1, pairs - 1) as n:
                gather(2 * n + 4, 0, 2 * n + 3, n + 2)
                add_rows(2 * n, 0)
                gather(2 * n + 5, 1, 2 * n + 4, n + 2)
                add_rows(2 * n + 1, 1)
            for i in range(3):
                add_rows(last + i, i % 2)
            pool.wait_ge(s_ys, 16 * last + 48)

        @block.scalar
        def _(act):
            act.dma_start(wv, wv_d.rearrange("p (k m) -> p k m", k=KC)).then_inc(s_wv, 16)
            for h in range(2):
                act.dma_start(ctxT[:, :, h * 256:(h + 1) * 256], ctxT_d[:, :, h * 256:(h + 1) * 256]).then_inc(s_ct[h], 16)
                if h == 0:
                    act.dma_start(wk, wk_d.rearrange("p (k m) -> p k m", k=KC)).then_inc(s_wk, 16)
            def copied(step, dst):
                n = TRN[step]
                act.wait_ge(s_tr, n + 1)
                act.copy(dst, ps[:, n % 2, :] if len(dst.shape) == 2 else
                         ps[:, n % 2, :].rearrange("p (k t) -> p k t", k=KC)).then_inc(s_trc, 1)

            def out_rows(j):
                act.wait_ge(s_x4, j + 1)
                act.dma_start(out_d[j * P:(j + 1) * P, :], xr[:, j, :]).then_inc(s_out, 16)

            for step in prog:
                kind = step[0]
                if kind == "a_prep":
                    j = step[1]
                    act.wait_ge(s_c[j], 16)
                    act.wait_ge(s_ncm, j + 1)
                    if j >= 2:
                        act.wait_ge(s_tr, TRN[("a_t", j - 2)] + 1)
                    act.activation(ek[:, j % 2, :], crow[:, j, :], ACT.Exp, bias=ncm[:, j:j + 1],
                                   accum_out=ksum[:, j:j + 1]).then_inc(s_ek, 1)
                elif kind == "a_q":
                    j = step[1]
                    act.wait_ge(s_x[j], 16)
                    act.wait_ge(s_nmr, j + 1)
                    if j >= 2:
                        act.wait_ge(s_a, j - 1)
                    act.activation(eq[:, j % 2, :], xr[:, j, :], ACT.Exp, bias=nmr[:, j:j + 1],
                                   scale=rstd[:, j:j + 1]).then_inc(s_eq, 1)
                elif kind == "a_t":
                    j = step[1]
                    if j >= 2:
                        act.wait_ge(s_kvs, j - 1)
                    copied(step, ekT[:, j % 2, :])
                elif kind == "ln_t":
                    copied(step, zT[:, :, step[2] * P:(step[2] + 1) * P])
                elif kind == "kv":
                    unit = step[1]
                    n = KVN[step]
                    bank = ps[:, 6 + n % 2, :]
                    act.wait_ge(s_pr, n + 1)
                    if unit[0] == "k":
                        _, t, h, _ = unit
                        bs = slice(8 * h, 8 * h + 8)
                        act.copy(kT[0:HD, t, bs, halves(unit)],
                                 bank[0:HD, :].rearrange("p (b s) -> p b s", b=8))
                        act.copy(kT[32 * t:32 * t + 32, 3, bs, halves(unit)],
                                 bank[HD:P, :].rearrange("p (b s) -> p b s", b=8)).then_inc(s_prc, 1)
                    else:
                        j = unit[1]
                        act.copy(v[halves(unit), 2 * j, :], bank[0:S, 0:G * HD])
                        act.copy(v[halves(unit), 2 * j + 1, :], bank[S:P, 0:G * HD]).then_inc(s_prc, 1)
                elif kind == "f_in":
                    h = step[1]
                    act.wait_ge(s_pt, h + 1)
                    act.copy(pT, ps[:, 7, :]).then_inc(s_ptc, 1)
                elif kind == "f_gu":
                    _, h, c = step
                    n = h * NF + c
                    m = P if c < NF - 1 else LASTF
                    if n == 0:
                        act.wait_ge(s_ffw, 6 * 16)
                    if n >= 2:
                        act.wait_ge(s_act, n - 1)
                    act.wait_ge(s_gu, n + 1)
                    act.activation(hs[0:m, n % 2, :], ps[0:m, 2 + n % 2, :], ACT.Silu,
                                   bias=b1[0:m, c:c + 1]).then_inc(s_sil, 1)
                elif kind == "f_oz":
                    act.wait_ge(s_oz, step[1] + 1)
                    act.copy(oz, ps[:, 6, :]).then_inc(s_ozc, 1)
                elif kind == "q":
                    _, q, g = step
                    act.wait_ge(s_q, 4 * q + g + 1)
                    act.copy(qT[0:HD, q % 2, :, 4 * g:4 * g + 3, :].rearrange("p b h s -> p h b s"),
                             ps[0:HD, 4:6, :].rearrange("p a b -> p (a b)")[:, 0:768]
                             .rearrange("p (h b s) -> p h b s", h=3, b=4)).then_inc(s_qca, 1)
                elif kind == "s":
                    n = step[1]
                    act.wait_ge(s_snm, n + 1)
                    if n >= 2:
                        act.wait_ge(s_tr, TRN[("t", n - 2)] + 1)
                    for u in range(4):
                        e = act.activation(prob[:, n % 2, u, :], ps[:, 2 + n % 2, u * P:(u + 1) * P], ACT.Exp,
                                           bias=snm[:, n % 4, u:u + 1], scale=SCALE,
                                           accum_out=ssum[:, n % 4, u:u + 1])
                    e.then_inc(s_p, 1)
                elif kind == "t":
                    n = step[1]
                    if n >= 2:
                        act.wait_ge(s_o, n - 1)
                    copied(step, probT[:, n % 2, :])
                elif kind == "gate":
                    j = step[1]
                    n = TRN[step]
                    act.wait_ge(s_tr, n + 1)
                    if j:
                        act.wait_ge(s_mk, j)
                    act.activation(gsc[:, 0, :], ps[:, n % 2, 0:E], ACT.Exp, scale=-1.0).then_inc(s_trc, 1)
                elif kind in ("place", "count"):
                    n = TRN[step]
                    act.wait_ge(s_tr, n + 1)
                    if kind == "count":
                        act.copy(nE, ps[:, n % 2, 0:E]).then_inc(s_trc, 1)
                    else:
                        if step[1]:
                            act.wait_ge(s_sl, step[1])
                        act.copy(pos[:, :], ps[:, n % 2, 0:E]).then_inc(s_trc, 1)
                elif kind == "sh_gu":
                    j = step[1]
                    act.wait_ge(s_hg, j + 1)
                    act.activation(sg[:, j % 2, :], ps[:, 4 + j % 2, 0:I], ACT.Silu).then_inc(s_hsil, 1)
                elif kind == "sh_t":
                    j = step[1]
                    act.wait_ge(s_ht, j + 1)
                    act.copy(zgT[:, j % 2, :], ps[:, 2 + j % 2, 0:I]).then_inc(s_htc, 1)
                elif kind == "ids":
                    act.wait_ge(s_idt, 1)
                    act.copy(ids[:, 0:P], ps[:, 0, 0:P])
                    act.copy(wts[:, 0:P], ps[:, 0, P:2 * P]).then_inc(s_ids, 1)
                elif kind == "sh_d" and step[1] >= 3:
                    out_rows(step[1] - 3)

            def x_copy(i, par):
                act.wait_ge(s_tx, i + 1)
                act.copy(xT[:, par, :], ps[:, par, :]).then_inc(s_txc, 1)

            def z_copy(i, par):
                act.wait_ge(s_tz, i + 1)
                act.copy(zgT[:, par, :], ps[:, 2 + par, 0:I]).then_inc(s_tzc, 1)

            def silu(i, par):
                act.wait_ge(s_eg, i + 1)
                act.activation(sg[:, par, :], ps[:, 4 + par, 0:I], ACT.Silu).then_inc(s_esil, 1)

            act.wait_ge(s_tabl, 1)
            pairs = act.value_load(tab[0:1, 193:194], min_val=16, max_val=TILES // 2)

            def act_step(i, par):
                x_copy(i + 1, 1 - par)
                if not isinstance(i, int) or i:
                    z_copy(i - 1, 1 - par)
                silu(i, par)

            x_copy(0, 0)
            for i in range(5):
                act_step(i, i % 2)
            with act.Fori(3, 2 * pairs - 2, 2) as n:
                act_step(n + 2, 1)
                act_step(n + 3, 0)
            z_copy(2 * pairs, 0)

        @block.vector
        def _(dve):
            count = [0]

            def link(ins):
                count[0] += 1
                ins.then_inc(chain_v, 1)
                dve.wait_ge(chain_v, count[0])

            def probs(n):
                dve.wait_ge(s_p, n + 1)
                link(dve.reciprocal(srs[:, n % 4, :], ssum[:, n % 4, :]))
                dve.tensor_tensor(prob[:, n % 2, :, :], prob[:, n % 2, :, :],
                                  srs[:, n % 4, :].rearrange("p (u a) -> p u a", a=1).to_broadcast((P, 4, P)),
                                  ALU.mult).then_inc(s_pn, 1)

            def pick(row, j, to):
                link(dve.tensor_tensor(ohs[:, :, :], onehot[:, j, :, :],
                                       row.rearrange("p (a e) -> p a e", a=1).to_broadcast((P, TOPK, E)), ALU.mult))
                link(dve.tensor_reduce(to, ohs[:, :, :], AX_X, ALU.add))

            nt, used, endT, startT, ordi, ordx, skip, one, tmp = (tb[:, i, :] for i in range(1, 10))

            def rows(a, n):
                return a.rearrange("p (a e) -> p a e", a=1).to_broadcast((P, n, E))

            def cols(a, n):
                return a.rearrange("p (n a) -> p n a", a=1).to_broadcast((P, n, E))

            def grid(i, n):
                return tt[:, i, 0:n * E].rearrange("p (n e) -> p n e", e=E)

            def route(part):
                if part == 0:
                    route_loads()
                elif part == 1:
                    route_tiles()
                else:
                    route_weights()

            def route_loads():
                dve.wait_ge(s_trc, TRN[("count",)] + 1)
                link(dve.memset(one, 1.0))
                g8 = tt[:, 0, 0:E * 8].rearrange("p (e m) -> p e m", m=8)
                link(dve.tensor_tensor(g8, nE.rearrange("p (e a) -> p e a", a=1).to_broadcast((P, E, 8)),
                                       m128.rearrange("p (a m) -> p a m", a=1).to_broadcast((P, E, 8)), ALU.is_gt))
                link(dve.tensor_reduce(nt, g8, AX_X, ALU.add))
                link(dve.tensor_scalar(used, nt, 0.0, None, ALU.is_gt))
                link(dve.tensor_tensor_scan(endT, one, nt, 0.0, ALU.mult, ALU.add))
                link(dve.tensor_tensor_scan(ordi, one, used, 0.0, ALU.mult, ALU.add))
                link(dve.tensor_tensor(startT, endT, nt, ALU.subtract))
                link(dve.tensor_tensor(ordx, ordi, used, ALU.subtract))
                link(dve.tensor_tensor(grid(0, E), rows(ordx, E), cols(iota16, E), ALU.is_equal))
                link(dve.tensor_tensor(grid(0, E), grid(0, E), rows(used, E), ALU.mult))
                link(dve.tensor_tensor(grid(0, E), grid(0, E), rows(iota16, E), ALU.mult))
                link(dve.tensor_reduce(tf[:, 144:160], grid(0, E), AX_X, ALU.add))
                link(dve.tensor_scalar(tmp, ordx, float(RING), None, ALU.add))
                link(dve.tensor_tensor(grid(1, E), rows(tmp, E), cols(iota16, E), ALU.is_equal))
                link(dve.tensor_tensor(tmp, endT, used, ALU.mult))
                link(dve.tensor_tensor(grid(1, E), grid(1, E), rows(tmp, E), ALU.mult))
                link(dve.tensor_reduce(tf[:, 160:176], grid(1, E), AX_X, ALU.add))
                link(dve.tensor_copy(tf[:, 176:192], ringo))
                link(dve.tensor_copy(tf[:, 192:193], ordi[:, E - 1:E]))
                link(dve.tensor_scalar(tt[:, 2, 0:24], even24, endT[:, E - 1:E], None, ALU.is_le))
                link(dve.tensor_reduce(tf[:, 193:194], tt[:, 2, 0:24], AX_X, ALU.add))
                link(dve.tensor_scalar(tf[:, 194:195], tf[:, 193:194], 2.0, -2.0, ALU.mult, ALU.add))
                dve.tensor_copy(tab[:, 144:195], tf[:, 144:195]).then_inc(s_tabl, 1)

            def route_tiles():
                link(dve.memset(skip[:, 0:1], 0.0))
                link(dve.tensor_scalar(skip[:, 1:E], nt[:, 0:E - 1], -1.0, float(T // P), ALU.mult, ALU.add))
                link(dve.tensor_tensor(grid(0, 48), rows(startT, 48), cols(iota48, 48), ALU.is_le))
                link(dve.tensor_tensor(grid(1, 48), grid(0, 48), rows(skip, 48), ALU.mult))
                link(dve.tensor_reduce(tf[:, 0:48], grid(1, 48), AX_X, ALU.add))
                link(dve.tensor_tensor(tf[:, 0:48], tf[:, 0:48], iota48, ALU.add))
                behind = grid(2, 3)[:, :, :].rearrange("p n e -> p (n e)")
                link(dve.tensor_scalar(behind, iota48, endT[:, E - 1:E], float(P), ALU.is_ge, ALU.mult))
                link(dve.tensor_scalar(tf[:, 0:48], tf[:, 0:48], float(P), None, ALU.min))
                link(dve.tensor_tensor(tf[:, 0:48], tf[:, 0:48], behind, ALU.max))
                dve.tensor_copy(tab[:, 0:48], tf[:, 0:48]).then_inc(s_tabc, 1)

            def route_weights():
                link(dve.tensor_tensor(grid(0, 48), grid(0, 48), rows(used, 48), ALU.mult))
                link(dve.tensor_reduce(tf[:, 48:96], grid(0, 48), AX_X, ALU.add))
                load = tt[:, 1, 0:48]
                slots = tt[:, 2, 0:48]
                link(dve.tensor_scalar(load, tf[:, 48:96], -1.0, None, ALU.add))
                link(dve.tensor_copy(tf[:, 96:144], load))
                for full in range(RING, E, RING):
                    link(dve.tensor_scalar(slots, load, float(full), -float(RING), ALU.is_ge, ALU.mult))
                    link(dve.tensor_tensor(tf[:, 96:144], tf[:, 96:144], slots, ALU.add))
                link(dve.tensor_scalar(tf[:, 96:144], tf[:, 96:144], float(EW), None, ALU.mult))
                dve.tensor_copy(tab[:, 48:144], tf[:, 48:144]).then_inc(s_tab, 1)

            def stat(col, src):
                link(dve.bn_stats(st[:, col % 2, :], src))
                dve.bn_aggr(mv[:, col, :], st[:, col % 2, :]).then_inc(s_stat, 1)

            for step in prog:
                kind = step[0]
                if kind == "a_stat":
                    j = step[1]
                    dve.wait_ge(s_c[j], 16)
                    link(dve.tensor_reduce(cmx[:, j:j + 1], crow[:, j, :], AX_X, ALU.max))
                    dve.tensor_scalar(ncm[:, j:j + 1], cmx[:, j:j + 1], -1.0, None, ALU.mult).then_inc(s_ncm, 1)
                    dve.wait_ge(s_x[j], 16)
                    stat(j, xr[:, j, :])
                elif kind == "a_prep":
                    j = step[1]
                    dve.wait_ge(s_rstd, STN[("a_stat", j)] + 1)
                    dve.wait_ge(s_stat, STN[("a_stat", j)] + 1)
                    dve.scalar_tensor_tensor(nmr[:, j:j + 1], mv[:, j, 0:1], -1.0, rstd[:, j:j + 1],
                                             ALU.mult, ALU.mult).then_inc(s_nmr, 1)
                elif kind == "a_kvs":
                    j = step[1]
                    dve.wait_ge(s_ek, j + 1)
                    link(dve.reciprocal(krec[:, j:j + 1], ksum[:, j:j + 1]))
                    dve.wait_ge(s_kvs, j + 1)
                    if j == 0:
                        dve.wait_ge(s_cst, 16)
                    if j >= 2:
                        dve.wait_ge(s_a, j - 1)
                    dve.scalar_tensor_tensor(kvm[:, j % 2, :], ps[:, 2 + j % 2, 0:P], krec[:, j:j + 1], blk8,
                                             ALU.mult, ALU.mult).then_inc(s_kvm, 1)
                elif kind == "a_out":
                    j = step[1]
                    dve.wait_ge(s_a, j + 1)
                    link(dve.reciprocal(srec, ps[:, 5, :]))
                    if j:
                        dve.wait_ge(s_x1, j)
                    dve.tensor_tensor(sout, ps[:, 4, :], srec, ALU.mult).then_inc(s_ac, 1)
                elif kind == "ln_stat":
                    _, layer, j = step
                    if layer == 1:
                        dve.wait_ge(s_x1, j + 1)
                    else:
                        dve.wait_ge(s_x2 if layer == 2 else s_x3, j + 1)
                    stat(J * layer + j, xr[:, j, :])
                elif kind == "ln_z":
                    _, layer, j = step
                    n = LNN[step]
                    col = J * layer + j
                    dve.wait_ge(s_stat, STN[("ln_stat", layer, j)] + 1)
                    dve.wait_ge(s_rstd, STN[("ln_stat", layer, j)] + 1)
                    if n >= 2:
                        old = [p for p in prog if p[0] == "ln_z"][n - 2]
                        dve.wait_ge(s_tr, TRN[("ln_t", *old[1:])] + 1)
                        if old[1] == 3:
                            dve.wait_ge(s_zd, 16 * (old[2] + 1))
                    dve.tensor_scalar(zrow[:, n % 2, :], xr[:, j, :], mv[:, col, 0:1], rstd[:, col:col + 1],
                                      ALU.subtract, ALU.mult).then_inc(s_z, 1)
                elif kind == "f_gu":
                    _, h, c = step
                    n = h * NF + c
                    m = P if c < NF - 1 else LASTF
                    dve.wait_ge(s_sil, n + 1)
                    if n == 0:
                        dve.wait_ge(s_ffw, 6 * 16)
                    dve.scalar_tensor_tensor(ha[0:m, n % 2, :], ps[0:m, 4 + n % 2, :], b1[0:m, NF + c:NF + c + 1],
                                             hs[0:m, n % 2, :], ALU.add, ALU.mult).then_inc(s_act, 1)
                elif kind == "f_out":
                    j = step[1]
                    dve.wait_ge(s_xb, j + 1)
                    dve.wait_ge(s_fo, j + 1)
                    dve.tensor_tensor(xr[:, j, :], ps[:, 6 + j % 2, :], xr[:, j, :], ALU.add).then_inc(s_x2, 1)
                elif kind == "q":
                    _, q, g = step
                    dve.wait_ge(s_q, 4 * q + g + 1)
                    for t in range(3):
                        c = dve.tensor_copy(qT[32 * t:32 * t + 32, q % 2, :, 4 * g + 3, :],
                                            ps[HD:P, 4 + t // 2, 256 * (t % 2):256 * (t % 2) + 256]
                                            .rearrange("p (b s) -> p b s", b=4))
                    c.then_inc(s_qcv, 1)
                elif kind == "s":
                    n = step[1]
                    dve.wait_ge(s_s, n + 1)
                    if n >= 4:
                        dve.wait_ge(s_p, n - 3)
                    link(dve.tensor_reduce(smx[:, n % 4, :], ps[:, 2 + n % 2, :].rearrange("p (u s) -> p u s", u=4),
                                           AX_X, ALU.max))
                    dve.tensor_scalar(snm[:, n % 4, :], smx[:, n % 4, :], -SCALE, None, ALU.mult).then_inc(s_snm, 1)
                elif kind == "pn":
                    probs(step[1])
                elif kind == "pv":
                    n = step[1]
                    b, hf = divmod(n, 2)
                    j = b // 2
                    side = slice(S * (b % 2), S * (b % 2) + S)
                    dve.wait_ge(s_o, n + 1)
                    if j >= 2 and b % 2 == 0 and hf == 0:
                        dve.wait_ge(s_op, j - 1)
                    src = ps[:, 6, :].rearrange("p (g h q) -> p g h q", g=2, h=HG)
                    dst = oT[:, j % 2, 6 * hf:6 * hf + 6, side].rearrange("p (g t) q -> p g t q", g=2)
                    for g in range(2):
                        dve.tensor_copy(dst[0:HD, g, :, :], src[0:HD, g, 0:3, :])
                    for t in range(3):
                        c = dve.tensor_copy(dst[HD:P, :, t, :], src[32 * t:32 * t + 32, :, 3, :])
                    c.then_inc(s_oc, 1)
                elif kind == "op1":
                    j = step[1]
                    dve.wait_ge(s_op, j + 1)
                    dve.tensor_tensor(xr[:, j, :], ps[:, 7, :], xr[:, j, :], ALU.add).then_inc(s_x3, 1)
                elif kind == "gate":
                    j = step[1]
                    if j == 0:
                        dve.wait_ge(s_small, 32)
                        dve.wait_ge(s_tables, 16)
                        dve.wait_ge(s_ms, 3)
                        link(dve.tensor_copy(tokw[:, :, :, 0],
                                             tokid[:, 0:J].rearrange("p (j a) -> p j a", a=1).to_broadcast((P, J, TOPK))))
                        link(dve.tensor_copy(ids[:, P:P + 1], tokid[:, J:J + 1]))
                        dve.memset(wts[:, P:P + 1], 0.0).then_inc(s_free, 1)
                    dve.wait_ge(s_trc, TRN[step] + 1)
                    link(dve.tensor_scalar(gsc[:, 1, :], gsc[:, 0, :], 1.0, None, ALU.add))
                    link(dve.reciprocal(gsc[:, 2, :], gsc[:, 1, :]))
                    link(dve.tensor_tensor(gsc[:, 3, :], gsc[:, 2, :], gb[:, :], ALU.add))
                    link(dve.max(top8[:, :], gsc[:, 3, :]))
                    link(dve.max_index(idx8[:, :], top8[:, :], gsc[:, 3, :]))
                    link(dve.tensor_copy(idxf[:, :], idx8[:, :]))
                    link(dve.tensor_tensor(onehot[:, j, :, :],
                                           idxf[:, 0:TOPK].rearrange("p (k a) -> p k a", a=1).to_broadcast((P, TOPK, E)),
                                           iota16.rearrange("p (a e) -> p a e", a=1).to_broadcast((P, TOPK, E)),
                                           ALU.is_equal))
                    link(dve.tensor_reduce(mask[:, j, :], onehot[:, j, :, :].rearrange("p k e -> p e k"), AX_X, ALU.add))
                    dve.tensor_tensor(mcum[:, j + 1, :], mcum[:, j, :], mask[:, j, :], ALU.add).then_inc(s_mk, 1)
                    link(dve.tensor_reduce(wsum[:, :], top8[:, 0:TOPK], AX_X, ALU.add))
                    link(dve.tensor_scalar(wsum[:, :], wsum[:, :], 1e-20, None, ALU.add))
                    link(dve.reciprocal(wsum[:, :], wsum[:, :]))
                    link(dve.tensor_scalar(tokw[:, j, :, 1], top8[:, 0:TOPK], wsum[:, 0:1], None, ALU.mult))
                elif kind == "place":
                    j = step[1]
                    dve.wait_ge(s_trc, TRN[step] + 1)
                    dve.wait_ge(s_mk, j + 1)
                    link(dve.tensor_tensor(slot[:, :], pos[:, :], iota16c, ALU.add))
                    pick(slot[:, :], j, slotf[:, :])
                    dve.tensor_copy(sloti[:, j, :], slotf[:, :]).then_inc(s_sl, 1)
                elif kind == "route":
                    route(step[1])
                elif kind == "sh_gu":
                    j = step[1]
                    dve.wait_ge(s_hsil, j + 1)
                    dve.tensor_tensor(zs[:, j, :], ps[:, 4 + j % 2, I:2 * I], sg[:, j % 2, :],
                                      ALU.mult).then_inc(s_hz, 1)
                elif kind == "sh_d":
                    j = step[1]
                    dve.wait_ge(s_hd, j + 1)
                    dve.wait_ge(s_x3, j + 1)
                    dve.tensor_tensor(xr[:, j, :], shared_down(j), xr[:, j, :], ALU.add).then_inc(s_x4, 1)

            def mul(i, par):
                dve.wait_ge(s_esil, i + 1)
                dve.tensor_tensor(zg[:, par, :], ps[:, 4 + par, I:2 * I], sg[:, par, :], ALU.mult).then_inc(s_ez, 1)

            def column(i):
                return dve.value_load(tab[0:1, bass.ds(i, 1)], min_val=0, max_val=P)

            def y_copy(i, par, added, col):
                dve.wait_ge(s_ed, i + 2)
                if added is not None:
                    dve.wait_ge(s_ys, 16 * added)
                dve.tensor_scalar(yrow[:, par, :], ps[:, 6 + par, :], wts[:, bass.ds(col, 1)], None,
                                  ALU.mult).then_inc(s_yc, 1)

            dve.wait_ge(s_tabl, 1)
            dve.wait_ge(s_ids, 1)
            pairs = dve.value_load(tab[0:1, 193:194], min_val=16, max_val=TILES // 2)
            for i in range(5):
                if i >= 2:
                    y_copy(i - 2, i % 2, i - 3 if i > 3 else None, column(i - 2))
                mul(i, i % 2)
            with dve.Fori(3, 2 * pairs - 2, 2) as n:
                for i, par in ((n + 2, 1), (n + 3, 0)):
                    col = column(i - 2)
                    y_copy(i - 2, par, n - 1 if par else n, col)
                    mul(i, par)
            last = dve.value_load(tab[0:1, 194:195], min_val=30, max_val=TILES - 3)
            for i in (1, 2):
                col = column(last + i)
                y_copy(last + i, i % 2, last + i - 1, col)

        @block.tensor
        def _(pe):
            pe.wait_ge(s_cst, 16)

            def tbank(step):
                n = TRN[step]
                if n >= 2:
                    pe.wait_ge(s_trc, n - 1)
                return ps[:, n % 2, :]

            def transposes(bank, src, n):
                for c in range(n):
                    mm = pe.transpose(bank[:, c * P:(c + 1) * P], src[:, c * P:(c + 1) * P], ident)
                return mm

            def normed(layer, j):
                pe.wait_ge(s_trc, TRN[("ln_t", layer, j)] + 1)

            def dense(out, lhs, rhs, n):
                for k in range(n):
                    mm = pe.matmul(out, lhs(k), rhs(k), start=(k == 0), stop=(k == n - 1))
                return mm

            for step in prog:
                kind = step[0]
                if kind == "a_t":
                    j = step[1]
                    pe.wait_ge(s_ek, j + 1)
                    transposes(tbank(step), ek[:, j % 2, :], KC).then_inc(s_tr, 1)
                elif kind == "a_kvs":
                    j = step[1]
                    pe.wait_ge(s_trc, TRN[("a_t", j)] + 1)
                    pe.wait_ge(s_ct[j // 2], 16)
                    if j >= 2:
                        pe.wait_ge(s_kvm, j - 1)
                    dense(ps[:, 2 + j % 2, 0:P], lambda k: ekT[:, j % 2, k * P:(k + 1) * P],
                          lambda k: ctxT[:, k, j * P:(j + 1) * P], KC).then_inc(s_kvs, 1)
                elif kind == "a_out":
                    j = step[1]
                    pe.wait_ge(s_kvm, j + 1)
                    pe.wait_ge(s_eq, j + 1)
                    if j:
                        pe.wait_ge(s_ac, j)
                    pe.matmul(ps[:, 4, :], kvm[:, j % 2, :], eq[:, j % 2, :], start=True, stop=True)
                    pe.matmul(ps[:, 5, :], blk8, eq[:, j % 2, :], start=True, stop=True).then_inc(s_a, 1)
                elif kind == "kv":
                    unit = step[1]
                    n = KVN[step]
                    lat = unit[-1]
                    src = zT if lat else ctxT
                    js = range(4 * unit[2], 4 * unit[2] + 4) if unit[0] == "k" else (unit[1],)
                    if n >= 2:
                        pe.wait_ge(s_prc, n - 1)
                    if n == len(ctx_units):
                        pe.wait_ge(s_x2, J)
                    if lat:
                        for j in js:
                            normed(2, j)
                    else:
                        for j in js[::2]:
                            pe.wait_ge(s_ct[j // 2], 16)
                    if unit[0] == "k":
                        pe.wait_ge(s_wk, 16)
                        t, h = unit[1:3]
                        dense(ps[:, 6 + n % 2, :], lambda k: wk[:, k, t * P:(t + 1) * P],
                              lambda k: src[:, k, h * 512:(h + 1) * 512], KC).then_inc(s_pr, 1)
                    else:
                        pe.wait_ge(s_wv, 16)
                        j = unit[1]
                        dense(ps[:, 6 + n % 2, 0:G * HD], lambda k: src[:, k, j * P:(j + 1) * P],
                              lambda k: wv[:, k, :], KC).then_inc(s_pr, 1)
                elif kind == "ln_t":
                    n = LNN[("ln_z", *step[1:])]
                    pe.wait_ge(s_z, n + 1)
                    transposes(tbank(step), zrow[:, n % 2, :], KC).then_inc(s_tr, 1)
                elif kind == "f_in":
                    h = step[1]
                    for j in range(4 * h, 4 * h + 4):
                        normed(1, j)
                    if h == 0:
                        pe.wait_ge(s_ffw, 6 * 16)
                        pe.wait_ge(s_prc, len(ctx_units))
                    else:
                        pe.wait_ge(s_ptc, 1)
                    dense(ps[:, 7, :], lambda k: u1[:, k, :], lambda k: zT[:, k, h * 512:(h + 1) * 512], KC)\
                        .then_inc(s_pt, 1)
                elif kind == "f_gu":
                    _, h, c = step
                    n = h * NF + c
                    m = P if c < NF - 1 else LASTF
                    pe.wait_ge(s_ptc, h + 1)
                    if n == 0:
                        pe.wait_ge(s_kvm, J)
                        pe.wait_ge(s_ac, J)
                    if n >= 2:
                        pe.wait_ge(s_act, n - 1)
                    pe.matmul(ps[0:m, 2 + n % 2, :], v1[:, c * P:c * P + m], pT, start=True, stop=True)
                    pe.matmul(ps[0:m, 4 + n % 2, :], v1[:, INTER + c * P:INTER + c * P + m], pT,
                              start=True, stop=True).then_inc(s_gu, 1)
                elif kind == "f_z":
                    _, h, c = step
                    n = h * NF + c
                    m = P if c < NF - 1 else LASTF
                    pe.wait_ge(s_act, n + 1)
                    if (h, c) == (1, 0):
                        pe.wait_ge(s_x2, 3)
                    mm = pe.matmul(ps[:, 6, :], u2[0:m, c, :], ha[0:m, n % 2, :], start=(c == 0), stop=(c == NF - 1))
                    if c == NF - 1:
                        mm.then_inc(s_oz, 1)
                elif kind == "f_out":
                    j = step[1]
                    pe.wait_ge(s_ozc, j // 4 + 1)
                    if j == 1:
                        pe.wait_ge(s_ptc, 2)
                    if j % 4 >= 2:
                        pe.wait_ge(s_x2, j - 1)
                    pe.matmul(ps[:, 6 + j % 2, :], oz[:, (j % 4) * P:(j % 4 + 1) * P], v2,
                              start=True, stop=True).then_inc(s_fo, 1)
                elif kind == "q":
                    _, q, g = step
                    n = 4 * q + g
                    if n == 0:
                        pe.wait_ge(s_wq, 16)
                        pe.wait_ge(s_act, 2 * NF)
                    else:
                        pe.wait_ge(s_qca, n)
                        pe.wait_ge(s_qcv, n)
                    normed(2, 2 * q)
                    normed(2, 2 * q + 1)
                    for t in range(3):
                        mm = dense(ps[:, 4 + t // 2, 256 * (t % 2):256 * (t % 2) + 256],
                                   lambda k: wq[:, k, (3 * g + t) * P:(3 * g + t + 1) * P],
                                   lambda k: zT[:, k, 256 * q:256 * q + 256], KC)
                    mm.then_inc(s_q, 1)
                elif kind == "s":
                    n = step[1]
                    b, hf = divmod(n, 2)
                    q = b // 4
                    if n == 0:
                        pe.wait_ge(s_prc, len(ctx_units) + 14)
                    pe.wait_ge(s_qca, 4 * q + 2 * hf + 2)
                    pe.wait_ge(s_qcv, 4 * q + 2 * hf + 2)
                    if n >= 2:
                        pe.wait_ge(s_p, n - 1)
                    for u in range(4):
                        g = 2 * hf + u // 2
                        h0 = 4 * g + 2 * (u % 2)
                        mm = pe.matmul(ps[:, 2 + n % 2, u * P:(u + 1) * P],
                                       qT[0:HD, q % 2, b % 4, h0:h0 + 2, :].rearrange("p h s -> p (h s)"), kT[0:HD, g, b, :],
                                       start=True, stop=True)
                    mm.then_inc(s_s, 1)
                elif kind == "t":
                    n = step[1]
                    pe.wait_ge(s_pn, n + 1)
                    transposes(tbank(step), prob[:, n % 2, :, :].rearrange("p u s -> p (u s)"), 4).then_inc(s_tr, 1)
                elif kind == "pv":
                    n = step[1]
                    b, hf = divmod(n, 2)
                    pe.wait_ge(s_trc, TRN[("t", n)] + 1)
                    if n:
                        pe.wait_ge(s_oc, n)
                    for g in range(2):
                        c0 = HD * (2 * hf + g)
                        mm = pe.matmul(ps[0:HD, 6, 256 * g:256 * g + 256], v[:, b, c0:c0 + HD],
                                       probT[:, n % 2, 256 * g:256 * g + 256], start=True, stop=True)
                    mm.then_inc(s_o, 1)
                elif kind in ("op0", "op1"):
                    j = step[1]
                    if kind == "op0":
                        pe.wait_ge(s_oc, 4 * j + 4)
                        if j == 0:
                            pe.wait_ge(s_wo, 16)
                        else:
                            pe.wait_ge(s_x3, j)
                    for m in range(NQT // 2 * int(kind[2]), NQT // 2 * (int(kind[2]) + 1)):
                        mm = pe.matmul(ps[:, 7, :], oT[:, j % 2, m, :], wo[:, m, :], start=(m == 0), stop=(m == NQT - 1))
                    if kind == "op1":
                        mm.then_inc(s_op, 1)
                elif kind == "gate":
                    j = step[1]
                    normed(3, j)
                    pe.wait_ge(s_small, 32)
                    dense(tbank(step)[:, 0:E], lambda k: zT[:, k, j * P:(j + 1) * P], lambda k: gw[:, k, :], KC)\
                        .then_inc(s_tr, 1)
                elif kind == "place":
                    j = step[1]
                    pe.wait_ge(s_mk, j + 1)
                    if j == 0:
                        pe.wait_ge(s_ms, 3)
                        pe.wait_ge(s_tables, 16)
                    bank = tbank(step)
                    pe.matmul(bank[:, 0:E], tri, mask[:, j, :], start=True, stop=False)
                    pe.matmul(bank[:, 0:E], ones, mcum[:, j, :], start=False, stop=True).then_inc(s_tr, 1)
                elif kind == "count":
                    pe.wait_ge(s_mk, J)
                    pe.matmul(tbank(step)[:, 0:E], ones, mcum[:, J, :], start=True, stop=True).then_inc(s_tr, 1)
                elif kind == "sh_gu":
                    j = step[1]
                    if j == 0:
                        pe.wait_ge(s_ws, 16)
                        pe.wait_ge(s_qca, 4 * G)
                        pe.wait_ge(s_qcv, 4 * G)
                    if j >= 2:
                        pe.wait_ge(s_hz, j - 1)
                    normed(3, j)
                    dense(ps[:, 4 + j % 2, :], lambda k: zT[:, k, j * P:(j + 1) * P],
                          lambda k: wsh[:, k * D:(k + 1) * D], KC).then_inc(s_hg, 1)
                elif kind == "sh_t":
                    j = step[1]
                    pe.wait_ge(s_hz, j + 1)
                    if j >= 2:
                        pe.wait_ge(s_htc, j - 1)
                    if j == 0:
                        pe.wait_ge(s_p, NU)
                    transposes(ps[:, 2 + j % 2, :], zs[:, j, :], I // P).then_inc(s_ht, 1)
                elif kind == "sh_d":
                    j = step[1]
                    pe.wait_ge(s_htc, j + 1)
                    if j == 0:
                        pe.wait_ge(s_oc, NU)
                        pe.wait_ge(s_x3, J)
                    if 2 <= j < J - 2:
                        pe.wait_ge(s_x4, j - 1)
                    dense(shared_down(j), lambda c: zgT[:, j % 2, c * P:(c + 1) * P],
                          lambda c: wsh[:, (KC + c) * D:(KC + c + 1) * D], I // P).then_inc(s_hd, 1)
                elif kind == "ids":
                    pe.wait_ge(s_idl, 16)
                    pe.wait_ge(s_trc, len(TRN))
                    for c in range(2):
                        mm = pe.transpose(ps[:, 0, c * P:(c + 1) * P], idrow[:, :, c], ident)
                    mm.then_inc(s_idt, 1)

            def up(sem, value):
                if not isinstance(value, int) or value > 0:
                    pe.wait_ge(sem, value)

            def rows_in(i, par):
                pe.wait_ge(s_gx[par], i * 8 + (16 if par == 0 else 8))
                up(s_txc, i - 1)
                transposes(ps[:, par, :], xrow[:, par, :], KC).then_inc(s_tx, 1)

            def slot_of(i):
                return pe.value_load(tab[0:1, bass.ds(i + 96, 1)], min_val=0, max_val=(RING - 1) * EW)

            def load_of(i):
                return pe.value_load(tab[0:1, bass.ds(i + 48, 1)], min_val=1, max_val=E)

            def gate_up(i, par, load, at):
                pe.wait_ge(s_w, load)
                pe.wait_ge(s_txc, i + 1)
                up(s_ez, i - 1)
                dense(ps[:, 4 + par, :], lambda k: xT[:, par, k * P:(k + 1) * P],
                      lambda k: ering[:, bass.ds(at + k * D, D)], KC).then_inc(s_eg, 1)

            def act_in(i, par, copied):
                pe.wait_ge(s_ez, i + 1)
                up(s_tzc, copied)
                transposes(ps[:, 2 + par, :], zg[:, par, :], I // P).then_inc(s_tz, 1)

            def down(i, par, copied, at):
                pe.wait_ge(s_tzc, i + 1)
                up(s_yc, copied)
                dense(ps[:, 6 + par, :], lambda c: zgT[:, par, c * P:(c + 1) * P],
                      lambda c: ering[:, bass.ds(at + (KC + c) * D, D)], I // P).then_inc(s_ed, 1)

            def pe_step(i, par):
                later = not isinstance(i, int)
                if later or i >= 2:
                    old = slot_of(i - 2)
                load, at = load_of(i), slot_of(i)
                if later or i >= 2:
                    down(i - 2, par, i - 3, old)
                rows_in(i + 1, 1 - par)
                if later or i:
                    act_in(i - 1, 1 - par, i - 2)
                gate_up(i, par, load, at)

            pe.wait_ge(s_tabl, 1)
            pe.wait_ge(s_tab, 1)
            pe.wait_ge(s_ids, 1)
            pe.wait_ge(s_x4, J)
            pe.sem_inc(s_ed, 1)
            rows_in(0, 0)
            for i in range(5):
                pe_step(i, i % 2)
            pairs = pe.value_load(tab[0:1, 193:194], min_val=16, max_val=TILES // 2)
            with pe.Fori(3, 2 * pairs - 2, 2) as n:
                pe_step(n + 2, 1)
                pe_step(n + 3, 0)
            last = pe.value_load(tab[0:1, 194:195], min_val=30, max_val=TILES - 3)
            old, at = slot_of(last + 1), slot_of(last + 2)
            down(last + 1, 1, last, old)
            act_in(last + 2, 0, last + 1)
            down(last + 2, 0, last + 1, at)


_INS = ["x", "ctx", "ctxT", "consts", "U1", "V1", "U2", "V2", "b1", "b2", "Wq", "Wk", "Wv", "Wo",
        "gate", "bias", "experts", "shared", "free_slots"]


def kernel(**inputs):
    import numpy as np
    import concourse.bacc as bacc
    from concourse import mybir as _mybir
    from concourse.bass_utils import run_bass_kernel_spmd as run

    a = {k: np.asarray(v) for k, v in inputs.items()}
    f = np.float32

    def chunks(w):
        n = w.shape[0] // P
        return np.ascontiguousarray(w.reshape(n, P, -1).transpose(1, 0, 2).reshape(P, -1))

    order = []
    for g in range(G):
        for t in range(3):
            order += [(g * HG + t) * HD + d for d in range(HD)]
            order += [(g * HG + 3) * HD + 32 * t + d for d in range(32)]
    korder = []
    for t in range(3):
        korder += [t * HD + d for d in range(HD)] + [3 * HD + 32 * t + d for d in range(32)]

    ctx = a["ctx_4096"].reshape(T, D)
    u2 = np.zeros((NF * P, RANK), f)
    u2[:INTER] = a["L0_ffn_U2"]
    b1 = np.zeros((2, NF * P), f)
    b1[:, :INTER] = a["L0_ffn_b1"].reshape(2, INTER)
    i = np.arange(P)
    cst = np.zeros((P, 4 * P + 176), f)
    cst[:, 0:P] = np.eye(P)
    cst[:, P:2 * P] = (i[:, None] // DH == i[None, :] // DH)
    cst[:, 2 * P:3 * P] = (i[:, None] < i[None, :])
    cst[:, 3 * P:4 * P] = 1
    c0 = 4 * P
    cst[:, c0:c0 + 16] = np.arange(E)
    cst[:, c0 + 32:c0 + 48] = T * np.arange(E)
    cst[:, c0 + 48:c0 + 56] = P * np.arange(8)
    cst[:, c0 + 56:c0 + 72] = (np.arange(E) % RING) * EW
    cst[:, c0 + 72:c0 + 120] = np.arange(48)
    cst[:, c0 + 120:c0 + 144] = 2 * np.arange(1, 25)
    cst[:, c0 + 144:c0 + 153] = P * np.arange(J + 1)[None, :] + i[:, None]
    free = np.zeros((P, P, 2), f)
    free[:, :, 0] = T + i[None, :]

    def expert(g, u, d):
        gu = np.concatenate([g.T.reshape(KC, P, I), u.T.reshape(KC, P, I)], axis=2)
        return np.concatenate([gu.transpose(1, 0, 2).reshape(P, -1), chunks(d.T)], axis=1)

    host = {
        "x": a["x"].reshape(T, D), "ctx": ctx,
        "ctxT": ctx.T.reshape(KC, P, T).transpose(1, 0, 2),
        "consts": cst,
        "U1": chunks(a["L0_ffn_U1"]), "V1": a["L0_ffn_V1"], "U2": chunks(u2), "V2": a["L0_ffn_V2"],
        "b1": b1.reshape(2 * NF, P).T, "b2": a["L0_ffn_b2"].reshape(1, D),
        "Wq": chunks(a["L1_xattn_Wq"][order].T), "Wk": chunks(a["L1_xattn_Wk"][korder].T),
        "Wv": chunks(a["L1_xattn_Wv"].T), "Wo": chunks(a["L1_xattn_Wo"].T[order]),
        "gate": chunks(a["L1_ffn_gate_w"].T), "bias": a["L1_ffn_bias"].reshape(1, E),
        "experts": np.stack([expert(a["L1_ffn_Wg"][e], a["L1_ffn_Wu"][e], a["L1_ffn_Wd"][e]) for e in range(E)]),
        "free_slots": free.reshape(P, 2 * P),
        "shared": expert(a["L1_ffn_Sg"], a["L1_ffn_Su"], a["L1_ffn_Sd"]),
    }
    nc = bacc.Bacc("TRN2", target_bir_lowering=False, num_devices=1)
    arrays, args = {}, []
    for name in _INS:
        arr = np.ascontiguousarray(host[name])
        arrays[f"in_{name}"] = arr
        args.append(nc.dram_tensor(f"in_{name}", arr.shape, _mybir.dt.from_np(arr.dtype), kind="ExternalInput").ap())
    out = nc.dram_tensor("out", (T + P, D), F32, kind="ExternalOutput").ap()
    build(nc, *args, out)
    r = run(nc, [arrays], core_ids=[0])
    return r.results[0]["out"][:T].reshape(B, S, D)
```
